# Optimizing a Trainium2 kernel written in Bass

```python
import numpy as np
import jax
import jax.numpy as jnp

def _softmax(x, axis=-1):
    return jax.nn.softmax(x, axis=axis)

def _gelu(x):
    return jax.nn.gelu(x, approximate=True)

def _silu(x):
    return jax.nn.silu(x)

def _sigmoid(x):
    return jax.nn.sigmoid(x)

def _layernorm(x, axis=-1, eps=1e-05):
    m = jnp.mean(x, axis=axis, keepdims=True)
    v = jnp.var(x, axis=axis, keepdims=True)
    return (x - m) / jnp.sqrt(v + eps)

def _scatter_add(tgt, idx, src, axis=0):
    return tgt.at[idx].add(src)

def _segment_sum(src, seg, n):
    return jax.ops.segment_sum(src, seg, n)
kernel_name = 'mk_xattn_seq_d1_seqx_r8_ae25a0'

def setup_inputs(seed: int=0):
    np.random.seed(seed)
    _w = jnp.asarray

    def _rec_inputs():
        import jax
        import jax.numpy as jnp
        _rk = jax.random.key(seed)
        x = 7.22e-05 + 1 * jax.random.normal(jax.random.fold_in(_rk, 1), (64, 64, 128), jnp.float32)
        _lenS = 64 - jax.random.randint(jax.random.fold_in(_rk, 7), (64,), 0, max(1, 64 // 4) + 1, jnp.int32)
        _lenS2 = 64 - jax.random.randint(jax.random.fold_in(_rk, 8), (64,), 0, max(1, 64 // 4) + 1, jnp.int32)
        _ctx_768P = jax.random.normal(jax.random.fold_in(_rk, 11), (64, 16, 96), jnp.float32)
        _ctx_768c = jax.random.dirichlet(jax.random.fold_in(_rk, 511), 0.3 * jnp.ones((16,), jnp.float32), (64, 64))
        _ctx_768t = jnp.einsum('bsk,bkd->bsd', _ctx_768c, _ctx_768P)
        _ctx_768t = _ctx_768t * jax.lax.rsqrt(jnp.mean(jnp.square(_ctx_768t)) + 1e-12) * 0.953939
        ctx_768 = 0.000651243 + 0.998673 * (_ctx_768t + 0.3 * jax.random.normal(jax.random.fold_in(_rk, 611), (64, 64, 96), jnp.float32))
        return (x, ctx_768)
    x, ctx_768 = _rec_inputs()

    def _L0_xattn_setup():
        import jax, jax.numpy as jnp
        import numpy as np
        HEADS = 16
        D_HEAD = 64
        EPS = 1e-05

        def _ln(x, g, b):
            m = jnp.mean(x, axis=-1, keepdims=True)
            v = jnp.var(x, axis=-1, keepdims=True)
            return (x - m) * jax.lax.rsqrt(v + EPS) * g + b

        def _attn(xq, xc, Wq, Wk, Wv, Wo, bo):
            B, N, _ = xq.shape
            S = xc.shape[1]
            q = (xq @ Wq).reshape(B, N, HEADS, D_HEAD)
            k = (xc @ Wk).reshape(B, S, HEADS, D_HEAD)
            v = (xc @ Wv).reshape(B, S, HEADS, D_HEAD)
            scale = D_HEAD ** (-0.5)
            scores = jnp.einsum('bnhd,bshd->bhns', q, k) * scale
            attn = jax.nn.softmax(scores, axis=-1)
            out = jnp.einsum('bhns,bshd->bnhd', attn, v).reshape(B, N, HEADS * D_HEAD)
            return out @ Wo + bo

        def _geglu_ff(x, Wp, bp, Wf, bf):
            h = x @ Wp + bp
            a, gate = jnp.split(h, 2, axis=-1)
            return a * jax.nn.gelu(gate, approximate=False) @ Wf + bf
        key = jax.random.key(seed)
        ks = jax.random.split(key, 16)
        dim, ctx, inner, ffin = (128, 96, HEADS * D_HEAD, 4 * 128)

        def w(k, i, o):
            return jax.random.normal(k, (i, o), jnp.float32) * i ** (-0.5)
        inp = {'x': jax.random.normal(ks[0], (4, 256, dim), jnp.float32), 'context': jax.random.normal(ks[1], (4, 77, ctx), jnp.float32), 'Wq1': w(ks[2], dim, inner), 'Wk1': w(ks[3], dim, inner), 'Wv1': w(ks[4], dim, inner), 'Wo1': w(ks[5], inner, dim), 'bo1': jnp.zeros((dim,), jnp.float32), 'Wq2': w(ks[6], dim, inner), 'Wk2': w(ks[7], ctx, inner), 'Wv2': w(ks[8], ctx, inner), 'Wo2': w(ks[9], inner, dim), 'bo2': jnp.zeros((dim,), jnp.float32), 'Wp': w(ks[10], dim, 2 * ffin), 'bp': jnp.zeros((2 * ffin,), jnp.float32), 'Wf': w(ks[11], ffin, dim), 'bf': jnp.zeros((dim,), jnp.float32), 'g1': jnp.ones((dim,), jnp.float32), 'b1': jnp.zeros((dim,), jnp.float32), 'g2': jnp.ones((dim,), jnp.float32), 'b2': jnp.zeros((dim,), jnp.float32), 'g3': jnp.ones((dim,), jnp.float32), 'b3': jnp.zeros((dim,), jnp.float32)}
        return inp
    _L0_xattn_all = _L0_xattn_setup()
    _L0_xattn_in = {k: v for k, v in _L0_xattn_all.items() if k in ('Wq1', 'Wk1', 'Wv1', 'Wo1', 'bo1', 'Wq2', 'Wk2', 'Wv2', 'Wo2', 'bo2', 'Wp', 'bp', 'Wf', 'bf', 'g1', 'b1', 'g2', 'b2', 'g3', 'b3')}
    del _L0_xattn_all
    return {'x': x, 'ctx_768': ctx_768, 'L0_xattn_Wq1': _L0_xattn_in['Wq1'], 'L0_xattn_Wk1': _L0_xattn_in['Wk1'], 'L0_xattn_Wv1': _L0_xattn_in['Wv1'], 'L0_xattn_Wo1': _L0_xattn_in['Wo1'], 'L0_xattn_bo1': _L0_xattn_in['bo1'], 'L0_xattn_Wq2': _L0_xattn_in['Wq2'], 'L0_xattn_Wk2': _L0_xattn_in['Wk2'], 'L0_xattn_Wv2': _L0_xattn_in['Wv2'], 'L0_xattn_Wo2': _L0_xattn_in['Wo2'], 'L0_xattn_bo2': _L0_xattn_in['bo2'], 'L0_xattn_Wp': _L0_xattn_in['Wp'], 'L0_xattn_bp': _L0_xattn_in['bp'], 'L0_xattn_Wf': _L0_xattn_in['Wf'], 'L0_xattn_bf': _L0_xattn_in['bf'], 'L0_xattn_g1': _L0_xattn_in['g1'], 'L0_xattn_b1': _L0_xattn_in['b1'], 'L0_xattn_g2': _L0_xattn_in['g2'], 'L0_xattn_b2': _L0_xattn_in['b2'], 'L0_xattn_g3': _L0_xattn_in['g3'], 'L0_xattn_b3': _L0_xattn_in['b3']}

def reference(x, ctx_768, L0_xattn_Wq1, L0_xattn_Wk1, L0_xattn_Wv1, L0_xattn_Wo1, L0_xattn_bo1, L0_xattn_Wq2, L0_xattn_Wk2, L0_xattn_Wv2, L0_xattn_Wo2, L0_xattn_bo2, L0_xattn_Wp, L0_xattn_bp, L0_xattn_Wf, L0_xattn_bf, L0_xattn_g1, L0_xattn_b1, L0_xattn_g2, L0_xattn_b2, L0_xattn_g3, L0_xattn_b3):
    import jax
    import jax.numpy as jnp

    def _L0_xattn_ref(x, context, Wq1, Wk1, Wv1, Wo1, bo1, Wq2, Wk2, Wv2, Wo2, bo2, Wp, bp, Wf, bf, g1, b1, g2, b2, g3, b3):
        import jax, jax.numpy as jnp
        import numpy as np
        HEADS = 16
        D_HEAD = 64
        EPS = 1e-05

        def _ln(x, g, b):
            m = jnp.mean(x, axis=-1, keepdims=True)
            v = jnp.var(x, axis=-1, keepdims=True)
            return (x - m) * jax.lax.rsqrt(v + EPS) * g + b

        def _attn(xq, xc, Wq, Wk, Wv, Wo, bo):
            B, N, _ = xq.shape
            S = xc.shape[1]
            q = (xq @ Wq).reshape(B, N, HEADS, D_HEAD)
            k = (xc @ Wk).reshape(B, S, HEADS, D_HEAD)
            v = (xc @ Wv).reshape(B, S, HEADS, D_HEAD)
            scale = D_HEAD ** (-0.5)
            scores = jnp.einsum('bnhd,bshd->bhns', q, k) * scale
            attn = jax.nn.softmax(scores, axis=-1)
            out = jnp.einsum('bhns,bshd->bnhd', attn, v).reshape(B, N, HEADS * D_HEAD)
            return out @ Wo + bo

        def _geglu_ff(x, Wp, bp, Wf, bf):
            h = x @ Wp + bp
            a, gate = jnp.split(h, 2, axis=-1)
            return a * jax.nn.gelu(gate, approximate=False) @ Wf + bf
        x = _attn(_ln(x, g1, b1), _ln(x, g1, b1), Wq1, Wk1, Wv1, Wo1, bo1) + x
        x = _attn(_ln(x, g2, b2), context, Wq2, Wk2, Wv2, Wo2, bo2) + x
        x = _geglu_ff(_ln(x, g3, b3), Wp, bp, Wf, bf) + x
        return x
    x = _L0_xattn_ref(x, ctx_768, L0_xattn_Wq1, L0_xattn_Wk1, L0_xattn_Wv1, L0_xattn_Wo1, L0_xattn_bo1, L0_xattn_Wq2, L0_xattn_Wk2, L0_xattn_Wv2, L0_xattn_Wo2, L0_xattn_bo2, L0_xattn_Wp, L0_xattn_bp, L0_xattn_Wf, L0_xattn_bf, L0_xattn_g1, L0_xattn_b1, L0_xattn_g2, L0_xattn_b2, L0_xattn_g3, L0_xattn_b3)
    return x

_drawn_inputs = setup_inputs


def setup_inputs(seed=0):
    import zlib

    import numpy as np

    out = dict(_drawn_inputs(seed))
    spreads = {'L0_xattn_bo1': (0.0, 0.1),
     'L0_xattn_bo2': (0.0, 0.1),
     'L0_xattn_bp': (0.0, 0.1),
     'L0_xattn_bf': (0.0, 0.1),
     'L0_xattn_g1': (1.0, 0.2),
     'L0_xattn_b1': (0.0, 0.1),
     'L0_xattn_g2': (1.0, 0.2),
     'L0_xattn_b2': (0.0, 0.355),
     'L0_xattn_g3': (1.0, 0.2),
     'L0_xattn_b3': (0.0, 0.1)}
    factors = {}
    for name, (base, spread) in spreads.items():
        noise = np.random.default_rng([zlib.crc32(name.encode()), seed]).standard_normal(out[name].shape)
        drawn = base * np.exp(spread * noise) if base else spread * noise
        out[name] = jnp.asarray(drawn.astype(out[name].dtype))
    for name, factor in factors.items():
        out[name] = (out[name] * factor).astype(out[name].dtype)
    return out
```

```python
import concourse.bass as bass
from concourse import mybir
from concourse.alu_op_type import AluOpType as ALU
from contextlib import ExitStack


def xattn_block(nc, x, ctx_in, Wq1, Wk1, Wv1, Wo1, bo1, Wq2, Wk2, Wv2, Wo2, bo2, Wp, bp, Wf, bf,
                g1, b1, g2, b2, g3, b3, out):
    f32 = mybir.dt.float32
    f32r = mybir.dt.float32r
    ACT = mybir.ActivationFunctionType
    AX = mybir.AxisListType

    B, N, D = x.shape
    DC = ctx_in.shape[2]
    INNER = Wq1.shape[1]
    DH = 64
    H = INNER // DH
    HP = H // 2
    FF = Wf.shape[0]
    GB = 4
    PP = GB // 2
    GT = GB * N
    NG = B // GB
    NPAIR = B // 2
    SCALE = DH ** -0.5
    EPS = 1e-5
    HALF = H // 2 * N
    TF = H * GT // 512
    NCH = FF // 128
    PARTS = ((0, 0), (1, 0), (0, 1))
    DK = (D, DC)
    A2, FFK = NG, 2 * NG
    KEND = 3 * NG

    stack = ExitStack()
    with stack:
        def sb(name, shape, dt=f32):
            return stack.enter_context(nc.sbuf_tensor(name, shape, dt))

        def sem(name):
            return stack.enter_context(nc.semaphore(name))

        xs = sb("xs", [128, NPAIR, D])
        ident = sb("ident", [128, 128])
        AW = [[sb(f"AW{a}{s}", [128, H, D], f32r) for s in "hl"] for a in range(2)]
        OW = [[sb(f"OW{a}{s}", [128, H, D], f32r) for s in "hl"] for a in range(2)]
        wp_raw = sb("wp_raw", [128, 2 * FF])
        wf_raw = sb("wf_raw", [128, NCH, D])
        gam = sb("gam", [128, 3, D])
        bet = sb("bet", [128, 3, D])
        bo_col = sb("bo_col", [128, 3])
        bp_col = sb("bp_col", [128, 2 * NCH])
        xt = [[sb(f"xt{k}{s}", [128, PP, 4 * 64], f32r) for s in "hl"] for k in range(2)]
        kd = [[sb(f"kd{k}{s}", [128, GB, 128], f32r) for s in "hl"] for k in range(2)]
        kn = sb("kn", [128, PP, D])
        cx = [sb(f"cx{k}", [128, GB, DC]) for k in range(2)]
        ct = [sb(f"ct{s}", [128, GT], f32r) for s in "hl"]
        P = [sb(f"P{p}", [128, H * N]) for p in range(PP)]
        pt = [sb(f"pt{s}", [128, HP, 128], f32r) for s in "hl"]
        xz = sb("xz", [128, PP, D])
        xg = sb("xg", [128, PP, D])
        xn = sb("xn", [128, PP, D])
        oT = sb("oT", [128, GT])
        stats = sb("stats", [128, PP, 6])
        mv = sb("mv", [128, PP, 2])
        veps = sb("veps", [128, PP])
        rstd = sb("rstd", [128, PP])
        neghalf = sb("neghalf", [128, PP])
        epsc = sb("epsc", [128, PP])
        one = sb("one", [128, 1])
        mx = sb("mx", [128, PP, H])
        sm = sb("sm", [128, PP, H])
        rs = sb("rs", [128, PP, H])

        with ExitStack() as region:
            def rb(name, shape, dt=f32):
                return region.enter_context(nc.sbuf_tensor(name, shape, dt))
            wst = [[rb(f"wst{a}{w}", [128, INNER]) for w in "kqv"] for a in range(2)]
            wo_st = [rb(f"wo_st{a}", [128, HP, D]) for a in range(2)]
            wT = [[rb(f"wT{a}{w}", [128, HP, 128]) for w in "kqv"] for a in range(2)]
        with ExitStack() as region:
            T = [rb(f"T{s}", [128, GB, H, N], f32r) for s in "hl"]
            U = [rb(f"U{s}", [128, H, GT], f32r) for s in "hl"]
        with ExitStack() as region:
            wp = [rb(f"wp{s}", [128, 2 * FF], f32r) for s in "hl"]
            wf = [rb(f"wf{s}", [128, NCH, D], f32r) for s in "hl"]
            gel = rb("gel", [128, NCH, GT])
            yf = rb("yf", [128, NCH, GT])
            yh = [rb(f"y{s}", [128, NCH, GT], f32r) for s in "hl"]

        ps_s = [stack.enter_context(nc.psum_tensor(f"ps_s{i}", [128, 512], f32)) for i in range(2)]
        ring = [stack.enter_context(nc.psum_tensor(f"ring{i}", [128, 512], f32)) for i in range(5)]
        ps_m = stack.enter_context(nc.psum_tensor("ps_m", [128, 512], f32))

        w_in = [[sem(f"w_in{a}{w}") for w in "kqvo"] for a in range(2)]
        x_in = [sem(f"x_in{i}") for i in range(4)]
        c_in = sem("c_in")
        ff_in = sem("ff_in")
        cx_in = [sem(f"cx_in{k}") for k in range(2)]
        consts = sem("consts")
        prep_fill = sem("prep_fill")
        prep_a = sem("prep_a")
        prep_v = sem("prep_v")
        st_done = sem("st_done")
        ln_var = sem("ln_var")
        eps_done = sem("eps_done")
        ln_rstd = sem("ln_rstd")
        ln_z = sem("ln_z")
        xg_done = sem("xg_done")
        xn_ready = sem("xn_ready")
        kn_hi = sem("kn_hi")
        kd_hi = sem("kd_hi")
        kd_ready = sem("kd_ready")
        xt_fill = sem("xt_fill")
        xt_hi = sem("xt_hi")
        xt_lo = sem("xt_lo")
        ct_hi = sem("ct_hi")
        ct_lo = sem("ct_lo")
        t_fill = sem("t_fill")
        t_hi = sem("t_hi")
        t_lo = sem("t_lo")
        s_fill = sem("s_fill")
        mx_done = sem("mx_done")
        s_sub = sem("s_sub")
        exp_done = sem("exp_done")
        sum_done = sem("sum_done")
        rs_done = sem("rs_done")
        p_norm = sem("p_norm")
        pt_fill = sem("pt_fill")
        pt_hi = sem("pt_hi")
        pt_lo = sem("pt_lo")
        u_fill = sem("u_fill")
        u_hi = sem("u_hi")
        u_lo = sem("u_lo")
        o_fill = sem("o_fill")
        o_out = sem("o_out")
        fin_fill = sem("fin_fill")
        fin_add = sem("fin_add")
        ffw_hi = sem("ffw_hi")
        ffw_lo = sem("ffw_lo")
        gate_fill = sem("gate_fill")
        gel_done = sem("gel_done")
        a_fill = sem("a_fill")
        y_done = sem("y_done")
        y_hi = sem("y_hi")
        y_lo = sem("y_lo")
        out_st = sem("out_st")

        def batches(t):
            return t[:, :, :].rearrange("d p (q c) -> d p q c", c=64)[:, :, 0:4:3, :]

        def pairs(K):
            return xs[:, bass.ds(PP * K, PP), :]

        def group_in_phase(K, a):
            return K - a * NG

        def prep_plan(a):
            first = (0, 1, 8, 9)
            return ([("T", 4 * q, wT[a][w]) for w in range(3) for q in range(2)]
                    + [("A", n, AW[a]) for n in first] + [("O", n, OW[a]) for n in first])

        def DKW(a, i):
            return (DK[a], D, DK[a])[i // 2]

        def T_BANK(K, i):
            return (8 * K + i) % 5

        def u_bank(p, c):
            return ring[((2 if p == 0 else 16) + c) % 5]

        def u_src(p, c, a):
            return u_bank(p, c)[0:DK[a], :].rearrange("d (h n) -> d h n", n=N)

        def u_dst(s, p, c, a):
            t = 128 * p + 64 * (c // 2)
            return U[s][0:DK[a], c % 2:H:2, t:t + N]

        block = stack.enter_context(nc.Block())

        @block.sync
        def _(sp):
            xv = x.rearrange("(t b) n d -> (b n) t d", b=2)
            ov = out.rearrange("(t b) n d -> (b n) t d", b=2)

            def load_w(a, w, src):
                if w == 3:
                    sp.dma_start(wo_st[a][:, :, :], src.rearrange("(h p) d -> p h d", p=128)).then_inc(w_in[a][w], 16)
                else:
                    sp.dma_start(wst[a][w][0:src.shape[0], :], src).then_inc(w_in[a][w], 16)

            load_w(0, 0, Wk1)
            load_w(0, 1, Wq1)
            for g in range(3):
                sp.dma_start(xs[:, PP * g:PP * g + PP, :], xv[:, PP * g:PP * g + PP, :]).then_inc(x_in[g], 16)
            load_w(0, 2, Wv1)
            load_w(0, 3, Wo1)
            sp.dma_start(xs[:, 3 * PP:NPAIR, :], xv[:, 3 * PP:NPAIR, :]).then_inc(x_in[3], 16)
            load_w(1, 0, Wk2)
            load_w(1, 1, Wq2)
            load_w(1, 2, Wv2)
            load_w(1, 3, Wo2)
            sp.dma_start(wp_raw[:, :], Wp).then_inc(ff_in, 16)
            sp.dma_start(wf_raw[:, :, :], Wf.rearrange("(c p) d -> p c d", p=128)).then_inc(ff_in, 16)

            def load_context(k, buf, first):
                if not first:
                    sp.wait_ge(kd_ready, 8 * (k + A2 - 1))
                    sp.wait_ge(xt_fill, k + A2 - 1)
                src = ctx_in[bass.ds(GB * k, GB), :, :].rearrange("b s d -> s b d")
                for r in (0, 64):
                    sp.dma_start(cx[buf][r:r + 64, :, :], src).then_inc(cx_in[buf], 16)

            load_context(0, 0, True)
            load_context(1, 1, True)
            with sp.Fori(1, NG // 2) as i:
                for c in range(2):
                    load_context(2 * i + c, c, False)

            def store(f):
                sp.wait_ge(fin_add, f + FFK + 1)
                sp.dma_start(ov[:, bass.ds(PP * f, PP), :], xs[:, bass.ds(PP * f, PP), :]).then_inc(out_st, 16)

            with sp.Fori(0, NG) as f:
                store(f)
            sp.wait_ge(out_st, 16 * NG)

        @block.gpsimd
        def _(pool):
            pool.memset(ident[:, :], 0.0).then_inc(consts, 1)
            for k in range(2):
                for s in range(2):
                    pool.memset(xt[k][s][:, :, :].bitcast(f32), 0.0).then_inc(consts, 1)
            pool.memset(neghalf[:, :], -0.5).then_inc(consts, 1)
            pool.memset(epsc[:, :], EPS).then_inc(consts, 1)
            pool.memset(one[:, :], 1.0).then_inc(consts, 1)
            pool.wait_ge(consts, 8)
            pool.affine_select(out=ident[:, :], in_=ident[:, :], compare_op=ALU.not_equal, fill=1.0,
                               base=0, pattern=[[-1, 128]], channel_multiplier=1).then_inc(consts, 1)
            for n, (g, b) in enumerate(((g1, b1), (g2, b2), (g3, b3))):
                pool.dma_start(gam[:, n, :], g.partition_broadcast(128)).then_inc(c_in, 16)
                pool.dma_start(bet[:, n, :], b.partition_broadcast(128)).then_inc(c_in, 16)
            for n, b in enumerate((bo1, bo2, bf)):
                pool.dma_start(bo_col[:, n:n + 1], b.rearrange("(d o) -> d o", o=1)).then_inc(c_in, 16)
            pool.dma_start(bp_col[:, :], bp.rearrange("(c p) -> p c", p=128),
                           allow_slow_non_contiguous=True).then_inc(c_in, 16)
            pool.wait_ge(c_in, 160)

            def inverse_std(K, first=False):
                pool.wait_ge(ln_var, 2 * K + 2)
                pool.tensor_tensor(veps[:, :], mv[:, :, 1], epsc[:, :], ALU.add).then_inc(eps_done, 1)
                pool.wait_ge(eps_done, K + 1)
                pool.tensor_tensor(rstd[:, :], veps[:, :], neghalf[:, :], ALU.pow).then_inc(ln_rstd, 1)

            def gain_offset(K, ln, first=False):
                pool.wait_ge(ln_z, 2 * K + 2)
                gb = gam[:, ln:ln + 1, :].broadcast_to([128, PP, D])
                bb = bet[:, ln:ln + 1, :].broadcast_to([128, PP, D])
                pool.tensor_tensor(xg[:, :, :], xz[:, :, :], gb, ALU.mult).then_inc(xg_done, 1)
                pool.wait_ge(xg_done, K + 1)
                if not first:
                    pool.wait_ge(xt_fill, K)
                pool.tensor_tensor(xn[:, :, :], xg[:, :, :], bb, ALU.add).then_inc(xn_ready, 1)

            def key_hi(K, ln):
                pool.tensor_tensor(kn[:, :, :].bitcast(f32r), xg[:, :, :],
                                   bet[:, ln:ln + 1, :].broadcast_to([128, PP, D]), ALU.add).then_inc(kn_hi, 1)

            def key_copies(K, buf, a, first=False):
                if not first:
                    pool.wait_ge(u_fill, 8 * K - 8)
                if a == 0:
                    pool.wait_ge(kn_hi, K + 1)
                    pool.wait_ge(xn_ready, K + 1)
                    hi, lo = [t[:, :, :].rearrange("r (p b) d -> r p b d", b=2) for t in kd[buf]]
                    n = 0
                    for b in range(2):
                        rows = slice(64 * b, 64 * b + 64)
                        off = bet[rows, 0:1, :].broadcast_to([64, PP, D])
                        for r in (0, 64):
                            pool.tensor_tensor(hi[r:r + 64, :, b, :], xg[rows, :, :], off, ALU.add)\
                                .then_inc(kd_ready, 1)
                            pool.wait_ge(kd_ready, 8 * K + (n + 1))
                            pool.tensor_tensor(lo[r:r + 64, :, b, :], xn[rows, :, :], kn[rows, :, :],
                                               ALU.subtract).then_inc(kd_ready, 1)
                            pool.wait_ge(kd_ready, 8 * K + (n + 2))
                            n += 2
                else:
                    k = group_in_phase(K, 1)
                    pool.wait_ge(cx_in[buf], 16 * (k - buf) + 32)
                    pool.tensor_tensor(kd[buf][0][:, :, 0:DC], cx[buf][:, :, :],
                                       one[:, :].unsqueeze(2).broadcast_to([128, GB, DC]), ALU.mult).then_inc(kd_hi, 1)
                    pool.wait_ge(kd_hi, k + 1)
                    pool.tensor_tensor(kd[buf][1][:, :, 0:DC], cx[buf][:, :, :],
                                       kd[buf][0][:, :, 0:DC].bitcast(f32), ALU.subtract).then_inc(kd_ready, 8)

            def normalise(K, p):
                pool.wait_ge(rs_done, 2 * K + p + 1)
                v = P[p][:, :].rearrange("r (h s) -> r h s", h=H)
                pool.tensor_tensor(v, v, rs[:, p, :].unsqueeze(2).broadcast_to([128, H, N]), ALU.mult).then_inc(p_norm, 1)

            def norm_chain(K, ln, first=False):
                inverse_std(K, first)
                gain_offset(K, ln, first)
                if ln == 0:
                    key_hi(K, ln)

            def step(J, par, a_key, a_norm):
                normalise(J + 1, 0)
                normalise(J + 1, 1)
                key_copies(J + 2, par, a_key)
                norm_chain(J + 3, a_norm)

            norm_chain(0, 0, True)
            key_copies(0, 0, 0, True)
            norm_chain(1, 0)
            key_copies(1, 1, 0, True)
            norm_chain(2, 0)
            normalise(0, 0)
            normalise(0, 1)
            step(0, 0, 0, 0)
            with pool.Fori(0, 6) as i:
                for c in range(2):
                    step(2 * i + (c + 1), (c + 1) % 2, 0, 0)
            step(13, 1, 0, 1)
            step(14, 0, 1, 1)
            step(15, 1, 1, 1)
            with pool.Fori(0, 6) as i:
                for c in range(2):
                    step(2 * i + (c + 16), c % 2, 1, 1)
            step(28, 0, 1, 1)
            step(29, 1, 1, 2)
            normalise(31, 0)
            normalise(31, 1)
            norm_chain(33, 2)
            norm_chain(34, 2)
            pool.wait_ge(ff_in, 32)
            pool.wait_ge(s_fill, 4 * FFK)
            pool.wait_ge(o_fill, FFK)
            pool.tensor_copy(wp[0][:, :], wp_raw[:, :]).then_inc(ffw_hi, 1)
            pool.tensor_copy(wf[0][:, :, :], wf_raw[:, :, :]).then_inc(ffw_hi, 1)
            pool.wait_ge(ffw_hi, 2)
            pool.tensor_tensor(wp[1][:, :], wp_raw[:, :], wp[0][:, :].bitcast(f32), ALU.subtract).then_inc(ffw_lo, 1)
            pool.tensor_tensor(wf[1][:, :, :], wf_raw[:, :, :], wf[0][:, :, :].bitcast(f32),
                               ALU.subtract).then_inc(ffw_lo, 1)
            with pool.Fori(35, KEND) as K:
                norm_chain(K, 2)

        @block.scalar
        def _(act):
            for a in range(2):
                prep_banks = prep_plan(a)
                for i, (kind, n, dst) in enumerate(prep_banks):
                    m = 14 * a + i
                    act.wait_ge(prep_fill, m + 1)
                    if kind == "T":
                        act.activation(dst[:, n:n + 2, 0:DKW(a, i)],
                                       ring[m % 5][:, 0:2 * DKW(a, i)].rearrange("p (h d) -> p h d", h=2),
                                       ACT.Copy).then_inc(prep_a, 1)
                    else:
                        act.activation(dst[0][0:DK[a], n:n + 7:2, :],
                                       ring[m % 5][0:DK[a], :].rearrange("p (h d) -> p h d", h=4),
                                       ACT.Copy).then_inc(prep_a, 1)

            def xt_half(K, par, a, first=False):
                act.wait_ge(xt_fill, K + 1)
                if not first:
                    act.wait_ge(s_fill, 4 * K - 4)
                act.activation(batches(xt[par][0]), ps_m[:, 0:GT].rearrange("d (p q c) -> d p q c", q=2, c=64),
                               ACT.Copy).then_inc(xt_hi, 1)
                if a == 1:
                    act.wait_ge(t_fill, 8 * K)
                    act.activation(ct[0][0:DC, :], ps_m[0:DC, GT:2 * GT], ACT.Copy).then_inc(ct_hi, 1)

            def t_half(K, a, first=False):
                for i in range(TF):
                    act.wait_ge(t_fill, 8 * K + (i + 1))
                    if not first and i == 0:
                        act.wait_ge(s_fill, 4 * K)
                    bank = T_BANK(K, i) if first == 1 or first == 2 else (8 + i) % 5
                    act.activation(T[0][:, :, 2 * i:2 * i + 2, :].rearrange("d b h s -> d h b s"),
                                   ring[bank][:, :].rearrange("d (h b s) -> d h b s", h=2, b=GB),
                                   ACT.Copy).then_inc(t_hi, 1)

            def exps(K, p):
                for h in range(2):
                    act.wait_ge(s_sub, 4 * K + (2 * p + h + 1))
                    v = P[p][:, HALF * h:HALF * h + HALF]
                    act.activation(v, v, ACT.Exp, scale=SCALE).then_inc(exp_done, 1)

            def pt_half(K, p, first=False):
                for q in range(2):
                    act.wait_ge(pt_fill, 4 * K + (2 * p + q + 1))
                    if q == 0 and not (first and p == 0):
                        act.wait_ge(u_fill, 8 * K + 4 * p)
                    act.activation(pt[0][:, 4 * q:4 * q + 4, :],
                                   ring[(6 * p + q) % 5][:, :].rearrange("r (h c) -> r h c", h=4),
                                   ACT.Copy).then_inc(pt_hi, 1)

            def u_half(K, p, a, first=False):
                for c in range(4):
                    act.wait_ge(u_fill, 8 * K + (4 * p + c + 1))
                    if c == 0 and p == 0 and not first:
                        act.wait_ge(o_fill, K)
                    act.activation(u_dst(0, p, c, a), u_src(p, c, a), ACT.Copy).then_inc(u_hi, 1)

            def out_copy(K, a, src):
                act.wait_ge(o_fill, K + 1)
                if not (isinstance(K, int) and K == 0):
                    act.wait_ge(fin_fill, K)
                act.activation(oT[:, :], src, ACT.Identity, bias=bo_col[:, a:a + 1]).then_inc(o_out, 1)

            def step(J, par, a, a_next, a_norm, last=0):
                first = isinstance(J, int) and J == 0
                pt_half(J, 0, first)
                if last < 2:
                    exps(J + 1, 0)
                xt_half(J + 2, par, a_norm)
                u_half(J, 0, a, first)
                pt_half(J, 1)
                if last < 2:
                    exps(J + 1, 1)
                if last < 1:
                    t_half(J + 2, a_norm)
                u_half(J, 1, a)
                out_copy(J, a, ps_m[:, 0:GT])

            act.wait_ge(c_in, 160)
            xt_half(0, 0, 0, True)
            t_half(0, 0, 1)
            xt_half(1, 1, 0, True)
            exps(0, 0)
            exps(0, 1)
            t_half(1, 0, 2)
            step(0, 0, 0, 0, 0)
            with act.Fori(0, 6) as i:
                for c in range(2):
                    step(2 * i + (c + 1), (c + 1) % 2, 0, 0, 0)
            step(13, 1, 0, 0, 0)
            step(14, 0, 0, 0, 1)
            step(15, 1, 0, 1, 1)
            with act.Fori(0, 6) as i:
                for c in range(2):
                    step(2 * i + (c + 16), c % 2, 1, 1, 1)
            step(28, 0, 1, 1, 1)
            step(29, 1, 1, 1, 1)
            step(30, 0, 1, 1, 2, 1)
            step(31, 1, 1, 1, 2, 2)

            def ff_xt(K, par):
                act.wait_ge(xt_fill, K + 1)
                act.activation(batches(xt[par][0]), ring[2][:, 0:GT].rearrange("d (p q c) -> d p q c", q=2, c=64),
                               ACT.Copy).then_inc(xt_hi, 1)

            def gelus(f, first=False):
                for c in range(NCH):
                    act.wait_ge(gate_fill, 2 * f + (c // 2 + 1))
                    if not first:
                        act.wait_ge(y_done, 4 * f - (3 - c))
                    act.activation(gel[:, c, :], ps_s[c // 2][:, GT * (c % 2):GT * (c % 2) + GT], ACT.Gelu,
                                   bias=bp_col[:, NCH + c:NCH + c + 1]).then_inc(gel_done, 1)

            def y_half(f):
                act.wait_ge(y_done, 4 * f + 4)
                act.wait_ge(o_fill, f + FFK)
                act.activation(yh[0][:, :, :], yf[:, :, :], ACT.Copy).then_inc(y_hi, 1)

            def ff_step(f, par, first=False, turn=True, up=True):
                if up:
                    gelus(f, first)
                if not first:
                    out_copy(f + (FFK - 1), 2, ring[3][:, 0:GT])
                if turn:
                    ff_xt(f + (FFK + 2), par)
                if up:
                    y_half(f)

            ff_step(0, 0, True)
            ff_step(1, 1)
            with act.Fori(0, 6) as i:
                for c in range(2):
                    ff_step(2 * i + (c + 2), c)
            ff_step(14, 0, turn=False)
            ff_step(15, 1, turn=False)
            ff_step(16, 0, turn=False, up=False)

        @block.vector
        def _(dve):
            for a in range(2):
                for i, (kind, n, dst) in enumerate(prep_plan(a)):
                    m = 14 * a + i
                    if kind == "T":
                        dve.wait_ge(prep_a, m + 1)
                        w = DKW(a, i)
                        dve.tensor_copy(dst[:, n + 2:n + 4, 0:w],
                                        ring[m % 5][:, 2 * w:4 * w].rearrange("p (h d) -> p h d", h=2))\
                            .then_inc(prep_v, 1)
                    else:
                        dve.wait_ge(prep_a, m + 1)
                        dve.tensor_tensor(dst[1][0:DK[a], n:n + 7:2, :],
                                          ring[m % 5][0:DK[a], :].rearrange("p (h d) -> p h d", h=4),
                                          dst[0][0:DK[a], n:n + 7:2, :].bitcast(f32), ALU.subtract)\
                            .then_inc(prep_v, 1)

            def xrow(K, a, p):
                return xs[:, bass.ds(PP * (K - a * NG) + p, 1), :].rearrange("r o d -> r (o d)")

            def norm_stats(K, a, first=False):
                if a > 0:
                    dve.wait_ge(fin_add, K - (NG - 1))
                for p in range(PP):
                    dve.bn_stats(stats[:, p, :], xrow(K, a, p)).then_inc(st_done, 1)

            def norm_aggregate(K):
                for p in range(PP):
                    dve.bn_aggr(mv[:, p, :], stats[:, p, :]).then_inc(ln_var, 1)

            def norm_apply(K, a, first=False):
                dve.wait_ge(ln_rstd, K + 1)
                if not first:
                    dve.wait_ge(xg_done, K)
                for p in range(PP):
                    dve.tensor_scalar(xz[:, p, :], xrow(K, a, p), mv[:, p, 0:1], rstd[:, p:p + 1],
                                      ALU.subtract, ALU.mult).then_inc(ln_z, 1)

            def xt_rest(K, par, a, src):
                dve.wait_ge(xt_hi, K + 1)
                if a == 1:
                    dve.wait_ge(ct_hi, K - (A2 - 1))
                dve.tensor_tensor(batches(xt[par][1]), src[:, 0:GT].rearrange("d (p q c) -> d p q c", q=2, c=64),
                                  batches(xt[par][0]).bitcast(f32),
                                  ALU.subtract).then_inc(xt_lo, 1)
                if a == 1:
                    dve.tensor_tensor(ct[1][0:DC, :], ps_m[0:DC, GT:2 * GT], ct[0][0:DC, :].bitcast(f32),
                                      ALU.subtract).then_inc(ct_lo, 1)

            def t_rest(K, first=0):
                for i in range(TF):
                    dve.wait_ge(t_hi, 8 * K + (i + 1))
                    bank = T_BANK(K, i) if first else (8 + i) % 5
                    dst = [t[:, :, 2 * i:2 * i + 2, :].rearrange("d b h s -> d h b s") for t in T]
                    dve.tensor_tensor(dst[1], ring[bank][:, :].rearrange("d (h b s) -> d h b s", h=2, b=GB),
                                      dst[0].bitcast(f32), ALU.subtract).then_inc(t_lo, 1)

            def maxes(K, p, first=False):
                for h in range(2):
                    dve.wait_ge(s_fill, 4 * K + (2 * p + h + 1))
                    v = ps_s[h][:, :].rearrange("r (h s) -> r h s", s=N)
                    m = mx[:, p, HP * h:HP * h + HP]
                    dve.tensor_reduce(m, v, AX.X, ALU.max).then_inc(mx_done, 1)
                    dve.wait_ge(mx_done, 4 * K + (2 * p + h + 1))
                    if not first:
                        dve.wait_ge(pt_fill, 4 * K + (2 * p - 2))
                    dve.tensor_tensor(P[p][:, HALF * h:HALF * h + HALF].rearrange("r (h s) -> r h s", s=N), v,
                                      m.unsqueeze(2).broadcast_to([128, HP, N]), ALU.subtract).then_inc(s_sub, 1)

            def sums(K, p):
                dve.wait_ge(exp_done, 4 * K + (2 * p + 2))
                dve.tensor_reduce(sm[:, p, :], P[p][:, :].rearrange("r (h s) -> r h s", s=N), AX.X,
                                  ALU.add).then_inc(sum_done, 1)
                dve.wait_ge(sum_done, 2 * K + (p + 1))
                dve.reciprocal(rs[:, p, :], sm[:, p, :]).then_inc(rs_done, 1)

            def pt_rest(K, p):
                for q in range(2):
                    dve.wait_ge(pt_hi, 4 * K + (2 * p + q + 1))
                    dve.tensor_tensor(pt[1][:, 4 * q:4 * q + 4, :],
                                      ring[(6 * p + q) % 5][:, :].rearrange("r (h c) -> r h c", h=4),
                                      pt[0][:, 4 * q:4 * q + 4, :].bitcast(f32), ALU.subtract).then_inc(pt_lo, 1)

            def u_rest(K, p, a):
                for c in range(4):
                    dve.wait_ge(u_hi, 8 * K + (4 * p + c + 1))
                    dve.tensor_tensor(u_dst(1, p, c, a), u_src(p, c, a), u_dst(0, p, c, a).bitcast(f32),
                                      ALU.subtract).then_inc(u_lo, 1)

            def fin(K, a, src):
                dve.wait_ge(fin_fill, K + 1)
                v = pairs(K - a * NG)
                dve.tensor_tensor(v, src[:, 0:GT].rearrange("r (p d) -> r p d", p=PP), v, ALU.add)\
                    .then_inc(fin_add, 1)

            def step(J, par, a, a_next, a_norm, a_stats, last=0):
                first = isinstance(J, int) and J == 0
                pt_rest(J, 0)
                if last < 2:
                    maxes(J + 1, 0)
                if not first:
                    fin(J - 1, 1 if isinstance(J, int) and J - 1 >= NG else (0 if isinstance(J, int) else a), ps_m)
                xt_rest(J + 2, par, a_norm, ps_m)
                u_rest(J, 0, a)
                if last < 2:
                    sums(J + 1, 0)
                norm_stats(J + 3, a_stats)
                dve.wait_ge(st_done, 2 * J + 8)
                pt_rest(J, 1)
                norm_aggregate(J + 3)
                if last < 2:
                    maxes(J + 1, 1)
                if last < 1:
                    t_rest(J + 2)
                if last < 2:
                    sums(J + 1, 1)
                u_rest(J, 1, a)
                norm_apply(J + 3, a_stats)

            for g in range(3):
                dve.wait_ge(x_in[g], 16)
                norm_stats(g, 0)
                dve.wait_ge(st_done, 2 * g + 2)
                norm_aggregate(g)
                norm_apply(g, 0, g == 0)
                if g < 2:
                    xt_rest(g, g, 0, ps_m)
                if g == 0:
                    t_rest(0, 1)
            maxes(0, 0, True)
            maxes(0, 1, True)
            sums(0, 0)
            sums(0, 1)
            t_rest(1, 1)
            dve.wait_ge(x_in[3], 16)
            step(0, 0, 0, 0, 0, 0)
            with dve.Fori(0, 6) as i:
                for c in range(2):
                    step(2 * i + (c + 1), (c + 1) % 2, 0, 0, 0, 0)
            step(13, 1, 0, 0, 0, 1)
            step(14, 0, 0, 0, 1, 1)
            step(15, 1, 0, 1, 1, 1)
            step(16, 0, 1, 1, 1, 1)
            step(17, 1, 1, 1, 1, 1)
            with dve.Fori(0, 5) as i:
                for c in range(2):
                    step(2 * i + (c + 18), c % 2, 1, 1, 1, 1)
            step(28, 0, 1, 1, 1, 1)
            step(29, 1, 1, 1, 1, 2)
            step(30, 0, 1, 1, 2, 2, 1)
            step(31, 1, 1, 1, 2, 2, 2)
            fin(31, 1, ps_m)

            def products(f, first=False):
                for c in range(NCH):
                    dve.wait_ge(gel_done, 4 * f + (c + 1))
                    dve.wait_ge(a_fill, 2 * f + (c // 2 + 1))
                    if not first and c == 0:
                        dve.wait_ge(y_hi, f)
                        dve.wait_ge(y_lo, f)
                    dve.scalar_tensor_tensor(yf[:, c, :], ring[c // 2][:, GT * (c % 2):GT * (c % 2) + GT],
                                             bp_col[:, c:c + 1], gel[:, c, :], ALU.add, ALU.mult)\
                        .then_inc(y_done, 1)

            def y_rest(f):
                dve.wait_ge(y_hi, f + 1)
                dve.tensor_tensor(yh[1][:, :, :], yf[:, :, :], yh[0][:, :, :].bitcast(f32),
                                  ALU.subtract).then_inc(y_lo, 1)

            def ff_step(f, par, first=False, turn=True, stat=True, up=True, finish=True):
                if up:
                    products(f, first)
                if finish:
                    fin(f + (FFK - 2), 2, ring[4])
                if stat:
                    norm_stats(f + (FFK + 3), 2)
                    dve.wait_ge(st_done, 2 * f + (2 * FFK + 8))
                if turn:
                    xt_rest(f + (FFK + 2), par, 2, ring[2])
                if stat:
                    norm_aggregate(f + (FFK + 3))
                if up:
                    y_rest(f)
                if stat:
                    norm_apply(f + (FFK + 3), 2)

            ff_step(0, 0, True, finish=False)
            ff_step(1, 1, finish=False)
            with dve.Fori(0, 5) as i:
                for c in range(2):
                    ff_step(2 * i + (c + 2), c)
            ff_step(12, 0)
            ff_step(13, 1, stat=False)
            ff_step(14, 0, turn=False, stat=False)
            ff_step(15, 1, turn=False, stat=False)
            ff_step(16, 0, turn=False, stat=False, up=False)
            ff_step(17, 1, turn=False, stat=False, up=False)

        @block.tensor
        def _(pe):
            pe.wait_ge(consts, 9)
            for a in range(2):
                for i, (kind, n, dst) in enumerate(prep_plan(a)):
                    m = 14 * a + i
                    if m >= 5:
                        pe.wait_ge(prep_v, m - 4)
                    bank = ring[m % 5]
                    if kind == "T":
                        w = i // 2
                        pe.wait_ge(w_in[a][w], 16)
                        d = DKW(a, i)
                        for j in range(4):
                            last = pe.transpose(bank[:, d * j:d * j + d],
                                                wst[a][w][0:d, 128 * (n + j):128 * (n + j) + 128],
                                                ident[0:d, 0:d])
                    else:
                        if i == 6:
                            pe.wait_ge(prep_v, 14 * a + 4)
                        if i == 10:
                            pe.wait_ge(prep_v, 14 * a + 6)
                            pe.wait_ge(w_in[a][3], 16)
                        left = wT[a][0 if kind == "A" else 2]
                        right = wT[a][1] if kind == "A" else wo_st[a]
                        for j in range(4):
                            hp, r = (n + 2 * j) // 2, 64 * (n % 2)
                            last = pe.matmul(bank[0:DK[a], 128 * j:128 * j + 128], left[r:r + 64, hp, 0:DK[a]],
                                             right[r:r + 64, hp, :], start=True, stop=True)
                    last.then_inc(prep_fill, 1)

            def turn(K, par, a, bank, first=False):
                if a == 1:
                    k = K - A2
                    pe.wait_ge(cx_in[par], 16 * (k - par) + 32)
                pe.wait_ge(xn_ready, K + 1)
                if first:
                    if K > 0:
                        pe.wait_ge(xt_lo, K)
                else:
                    pe.wait_ge(fin_add, K - 2)
                for p in range(PP):
                    last = pe.transpose(bank[:, 128 * p:128 * p + 128], xn[:, p, :], ident[:, :])
                if a == 1:
                    for b in range(GB):
                        last = pe.transpose(bank[0:DC, GT + N * b:GT + N * b + N], cx[par][0:64, b, :],
                                            ident[0:64, 0:64])
                last.then_inc(xt_fill, 1)

            def t_products(K, par, a, first=0):
                pe.wait_ge(xt_lo, K + 1)
                if a == 1:
                    pe.wait_ge(ct_lo, K - (A2 - 1))
                mov = [batches(t) for t in xt[par]] if a == 0 else [t[0:DC, :] for t in ct]
                for i in range(TF):
                    if first:
                        bank = T_BANK(K, i)
                        n = 8 * K + i
                        if n >= 5:
                            pe.wait_ge(t_lo, n - 4)
                    else:
                        bank = (8 + i) % 5
                        if i < 3:
                            pe.wait_ge(u_lo, 8 * (K - 2) + (i + 2))
                        elif i < 5:
                            pe.wait_ge(pt_lo, 4 * (K - 2) + i)
                        else:
                            pe.wait_ge(t_lo, 8 * K + (i - 4))
                    for j in range(2):
                        o = ring[bank][:, GT * j:GT * j + GT]
                        for n, (s, m) in enumerate(PARTS):
                            last = pe.matmul(o, AW[a][s][0:DK[a], 2 * i + j, :], mov[m],
                                             start=(n == 0), stop=(n == 2))
                    last.then_inc(t_fill, 1)

            def scores(K, p, par, first=False):
                if p == 0:
                    pe.wait_ge(t_lo, 8 * K + 8)
                for h in range(2):
                    if not (first and p == 0):
                        pe.wait_ge(s_sub, 4 * K + (2 * p + h - 1))
                    n = 0
                    for b in range(2):
                        for s, m in PARTS:
                            last = pe.matmul(ps_s[h][:, :], xt[par][s][:, p, 128 * b:128 * b + 128],
                                             T[m][:, 2 * p + b, 8 * h:8 * h + 8, :].rearrange("d h s -> d (h s)"),
                                             start=(n == 0), stop=(n == 5))
                            n += 1
                    last.then_inc(s_fill, 1)

            def turn_softmax(K, p, with_t=True):
                pe.wait_ge(p_norm, 2 * K + (p + 1))
                if p == 0 and with_t:
                    pe.wait_ge(t_lo, 8 * K + 16)
                for q in range(2):
                    if p == 1 and q == 1:
                        pe.wait_ge(u_lo, 8 * K + 1)
                    for j in range(4):
                        hp = 4 * q + j
                        last = pe.transpose(ring[(6 * p + q) % 5][:, 128 * j:128 * j + 128],
                                            P[p][:, 128 * hp:128 * hp + 128], ident[:, :])
                    last.then_inc(pt_fill, 1)

            def u_products(K, p, par, a, with_t=True):
                pe.wait_ge(pt_lo, 4 * K + (2 * p + 2))
                pe.wait_ge(kd_ready, 8 * K + 8)
                for c in range(4):
                    b, r = c // 2, 64 * (c % 2)
                    if p == 1:
                        if with_t:
                            pe.wait_ge(t_lo, 8 * (K + 2) + (c + 4))
                        elif c == 0:
                            pe.wait_ge(u_lo, 8 * K + 4)
                    for n, (s, m) in enumerate(PARTS):
                        last = pe.matmul(u_src(p, c, a).rearrange("d h n -> d (h n)"),
                                         kd[par][s][r:r + 64, 2 * p + b, 0:DK[a]],
                                         pt[m][r:r + 64, :, 64 * b:64 * b + 64], start=(n == 0), stop=(n == 2))
                    last.then_inc(u_fill, 1)

            def out_products(K, a, turned=True):
                pe.wait_ge(u_lo, 8 * K + 8)
                pe.wait_ge(xt_lo, K + 3)
                if turned == 1:
                    pe.wait_ge(ct_lo, K - (A2 - 3))
                n = 0
                for h in range(H):
                    for s, m in PARTS:
                        last = pe.matmul(ps_m[:, 0:GT], OW[a][s][0:DK[a], h, :], U[m][0:DK[a], h, :],
                                         start=(n == 0), stop=(n == 3 * H - 1))
                        n += 1
                last.then_inc(o_fill, 1)

            def turn_back(K, bank):
                pe.wait_ge(o_out, K + 1)
                for p in range(PP):
                    last = pe.transpose(bank[:, 128 * p:128 * p + 128], oT[:, 128 * p:128 * p + 128], ident[:, :])
                last.then_inc(fin_fill, 1)

            def step(J, par, a, a_next, a_norm, last=0):
                first = isinstance(J, int) and J == 0
                turn_softmax(J, 0, last < 2)
                if last < 2:
                    scores(J + 1, 0, 1 - par)
                if not first:
                    turn_back(J - 1, ps_m)
                turn(J + 2, par, a_norm, ps_m, first)
                u_products(J, 0, par, a)
                turn_softmax(J, 1)
                if last < 2:
                    scores(J + 1, 1, 1 - par)
                if last < 1:
                    t_products(J + 2, par, a_norm)
                u_products(J, 1, par, a, last < 1)
                out_products(J, a, a_norm)

            pe.wait_ge(prep_v, 28)
            turn(0, 0, 0, ps_m, True)
            t_products(0, 0, 0, 1)
            turn(1, 1, 0, ps_m, True)
            scores(0, 0, 0, True)
            scores(0, 1, 0)
            t_products(1, 1, 0, 1)
            step(0, 0, 0, 0, 0)
            with pe.Fori(0, 6) as i:
                for c in range(2):
                    step(2 * i + (c + 1), (c + 1) % 2, 0, 0, 0)
            step(13, 1, 0, 0, 0)
            step(14, 0, 0, 0, 1)
            step(15, 1, 0, 1, 1)
            with pe.Fori(0, 6) as i:
                for c in range(2):
                    step(2 * i + (c + 16), c % 2, 1, 1, 1)
            step(28, 0, 1, 1, 1)
            step(29, 1, 1, 1, 1)
            step(30, 0, 1, 1, 2, 1)
            step(31, 1, 1, 1, 2, 2)
            turn_back(31, ps_m)

            def up_products(f, par, first=False):
                K = f + FFK
                pe.wait_ge(xt_lo, K + 1)
                mov = [batches(t) for t in xt[par]]
                for c in range(2 * NCH):
                    gate = c < NCH
                    i, j = (c % NCH) // 2, c % 2
                    if not first and j == 0:
                        if gate:
                            pe.wait_ge(gel_done, 4 * f - (2 - 2 * i))
                        else:
                            pe.wait_ge(y_done, 4 * f - (2 - 2 * i))
                    o = (ps_s if gate else ring)[i][:, GT * j:GT * j + GT]
                    col = 128 * (c % NCH) + (FF if gate else 0)
                    for n, (s, m) in enumerate(PARTS):
                        last = pe.matmul(o, wp[s][:, col:col + 128], mov[m], start=(n == 0), stop=(n == 2))
                    if j == 1:
                        last.then_inc(gate_fill if gate else a_fill, 1)

            def down_products(f):
                K = f + FFK
                pe.wait_ge(y_lo, f + 1)
                pe.wait_ge(o_out, K)
                n = 0
                for c in range(NCH):
                    for s, m in PARTS:
                        last = pe.matmul(ring[3][:, 0:GT], wf[s][:, c, :], yh[m][:, c, :],
                                         start=(n == 0), stop=(n == 3 * NCH - 1))
                        n += 1
                last.then_inc(o_fill, 1)

            def ff_turn(K):
                pe.wait_ge(xn_ready, K + 1)
                pe.wait_ge(xt_lo, K)
                for p in range(PP):
                    last = pe.transpose(ring[2][:, 128 * p:128 * p + 128], xn[:, p, :], ident[:, :])
                last.then_inc(xt_fill, 1)

            def ff_step(f, par, first=False, up=True, down=True, back=True, norm=True):
                if up:
                    up_products(f, par, first)
                if back:
                    K = f + (FFK - 2)
                    pe.wait_ge(fin_add, K)
                    turn_back(K, ring[4])
                if down:
                    down_products(f - 1)
                if norm:
                    ff_turn(f + (FFK + 2))

            pe.wait_ge(ffw_lo, 2)
            ff_step(0, 0, True, down=False, back=False)
            ff_step(1, 1, back=False)
            with pe.Fori(0, 6) as i:
                for c in range(2):
                    ff_step(2 * i + (c + 2), c)
            ff_step(14, 0, norm=False)
            ff_step(15, 1, norm=False)
            ff_step(16, 0, norm=False, up=False)
            ff_step(17, 1, norm=False, up=False, down=False)


_INS = ["x", "ctx_768"] + [f"L0_xattn_{n}" for n in
        ("Wq1", "Wk1", "Wv1", "Wo1", "bo1", "Wq2", "Wk2", "Wv2", "Wo2", "bo2", "Wp", "bp", "Wf", "bf",
         "g1", "b1", "g2", "b2", "g3", "b3")]


def kernel(**inputs):
    import numpy as _np
    import concourse.bacc as _bacc
    from concourse import mybir as _mybir
    from concourse.bass_utils import run_bass_kernel_spmd as _run

    nc = _bacc.Bacc("TRN2", target_bir_lowering=False, num_devices=1)
    arrays, args = {}, []
    for name in _INS:
        a = _np.ascontiguousarray(inputs[name])
        arrays[f"in_{name}"] = a
        args.append(nc.dram_tensor(f"in_{name}", a.shape, _mybir.dt.from_np(a.dtype), kind="ExternalInput").ap())
    o = nc.dram_tensor("out", arrays["in_x"].shape, _mybir.dt.from_np(arrays["in_x"].dtype),
                       kind="ExternalOutput").ap()
    xattn_block(nc, *args, o)
    r = _run(nc, [arrays], core_ids=[0])
    return r.results[0]["out"]
```

```python
import concourse.bass as bass
from concourse import mybir
from concourse.alu_op_type import AluOpType as ALU
from contextlib import ExitStack


def xattn_block(nc, x, ctx_in, Wq1, Wk1, Wv1, Wo1, bo1, Wq2, Wk2, Wv2, Wo2, bo2, Wp, bp, Wf, bf,
                g1, b1, g2, b2, g3, b3, out):
    f32 = mybir.dt.float32
    f32r = mybir.dt.float32r
    ACT = mybir.ActivationFunctionType
    AX = mybir.AxisListType

    B, N, D = x.shape
    DC = ctx_in.shape[2]
    INNER = Wq1.shape[1]
    DH = 64
    H = INNER // DH
    HP = H // 2
    FF = Wf.shape[0]
    GB = 4
    PP = GB // 2
    GT = GB * N
    NG = B // GB
    NPAIR = B // 2
    SCALE = DH ** -0.5
    EPS = 1e-5
    HALF = H // 2 * N
    TF = H * GT // 512
    NCH = FF // 128
    PARTS = ((0, 0), (1, 0), (0, 1))
    DK = (D, DC)
    A2, FFK = NG, 2 * NG
    KEND = 3 * NG

    stack = ExitStack()
    with stack:
        def sb(name, shape, dt=f32):
            return stack.enter_context(nc.sbuf_tensor(name, shape, dt))

        def sem(name):
            return stack.enter_context(nc.semaphore(name))

        xs = sb("xs", [128, NPAIR, D])
        ident = sb("ident", [128, 128])
        AW = [[sb(f"AW{a}{s}", [128, H, D], f32r) for s in "hl"] for a in range(2)]
        OW = [[sb(f"OW{a}{s}", [128, H, D], f32r) for s in "hl"] for a in range(2)]
        wp_raw = sb("wp_raw", [128, 2 * FF])
        wf_raw = sb("wf_raw", [128, NCH, D])
        gam = sb("gam", [128, 3, D])
        bet = sb("bet", [128, 3, D])
        bo_col = sb("bo_col", [128, 3])
        bp_col = sb("bp_col", [128, 2 * NCH])
        xt = [[sb(f"xt{k}{s}", [128, PP, 4 * 64], f32r) for s in "hl"] for k in range(2)]
        kd = [[sb(f"kd{k}{s}", [128, GB, 128], f32r) for s in "hl"] for k in range(2)]
        kn = sb("kn", [128, PP, D])
        cx = [sb(f"cx{k}", [128, GB, DC]) for k in range(2)]
        ct = [sb(f"ct{s}", [128, GT], f32r) for s in "hl"]
        P = [sb(f"P{p}", [128, H * N]) for p in range(PP)]
        pt = [sb(f"pt{s}", [128, HP, 128], f32r) for s in "hl"]
        xz = sb("xz", [128, PP, D])
        xg = sb("xg", [128, PP, D])
        xn = sb("xn", [128, PP, D])
        oT = sb("oT", [128, GT])
        stats = sb("stats", [128, PP, 6])
        mv = sb("mv", [128, PP, 2])
        veps = sb("veps", [128, PP])
        rstd = sb("rstd", [128, PP])
        neghalf = sb("neghalf", [128, PP])
        epsc = sb("epsc", [128, PP])
        one = sb("one", [128, 1])
        mx = sb("mx", [128, PP, H])
        sm = sb("sm", [128, PP, H])
        rs = sb("rs", [128, PP, H])

        with ExitStack() as region:
            def rb(name, shape, dt=f32):
                return region.enter_context(nc.sbuf_tensor(name, shape, dt))
            wst, wo_st, wT = [], [], []
            for a in range(2):
                wst.append([rb(f"wst{a}{w}", [128, INNER]) for w in "kqv"])
                wo_st.append(rb(f"wo_st{a}", [128, HP, D]))
                wT.append([rb(f"wT{a}{w}", [128, HP, 128]) for w in "kqv"])
                rb(f"spare{a}", [128, 2 * GB * H * N - 7 * INNER])
        with ExitStack() as region:
            T = [rb(f"T{s}", [128, GB, H, N], f32r) for s in "hl"]
            U = [rb(f"U{s}", [128, H, GT], f32r) for s in "hl"]
        with ExitStack() as region:
            wp = [rb(f"wp{s}", [128, 2 * FF], f32r) for s in "hl"]
            wf = [rb(f"wf{s}", [128, NCH, D], f32r) for s in "hl"]
            gel = rb("gel", [128, NCH, GT])
            yf = rb("yf", [128, NCH, GT])
            yh = [rb(f"y{s}", [128, NCH, GT], f32r) for s in "hl"]

        ps_s = [stack.enter_context(nc.psum_tensor(f"ps_s{i}", [128, 512], f32)) for i in range(2)]
        ring = [stack.enter_context(nc.psum_tensor(f"ring{i}", [128, 512], f32)) for i in range(5)]
        ps_m = stack.enter_context(nc.psum_tensor("ps_m", [128, 512], f32))

        w_in = [[sem(f"w_in{a}{w}") for w in "kqvo"] for a in range(2)]
        x_in = [sem(f"x_in{i}") for i in range(4)]
        c_in = sem("c_in")
        ff_in = sem("ff_in")
        cx_in = [sem(f"cx_in{k}") for k in range(2)]
        id_done = sem("id_done")
        consts = sem("consts")
        prep_fill = sem("prep_fill")
        prep_a = sem("prep_a")
        prep_v = sem("prep_v")
        st_done = sem("st_done")
        ln_var = sem("ln_var")
        eps_done = sem("eps_done")
        ln_rstd = sem("ln_rstd")
        ln_z = sem("ln_z")
        xg_done = sem("xg_done")
        xn_ready = sem("xn_ready")
        kn_hi = sem("kn_hi")
        kd_hi = sem("kd_hi")
        kd_ready = sem("kd_ready")
        xt_fill = sem("xt_fill")
        xt_hi = sem("xt_hi")
        xt_lo = sem("xt_lo")
        ct_hi = sem("ct_hi")
        ct_lo = sem("ct_lo")
        t_fill = sem("t_fill")
        t_hi = sem("t_hi")
        t_lo = sem("t_lo")
        s_fill = sem("s_fill")
        mx_done = sem("mx_done")
        s_sub = sem("s_sub")
        exp_done = sem("exp_done")
        sum_done = sem("sum_done")
        rs_done = sem("rs_done")
        p_norm = sem("p_norm")
        pt_fill = sem("pt_fill")
        pt_hi = sem("pt_hi")
        pt_lo = sem("pt_lo")
        u_fill = sem("u_fill")
        u_hi = sem("u_hi")
        u_lo = sem("u_lo")
        o_fill = sem("o_fill")
        o_out = sem("o_out")
        fin_fill = sem("fin_fill")
        fin_add = sem("fin_add")
        ffw_hi = sem("ffw_hi")
        ffw_lo = sem("ffw_lo")
        gate_fill = sem("gate_fill")
        gel_done = sem("gel_done")
        a_fill = sem("a_fill")
        y_done = sem("y_done")
        y_hi = sem("y_hi")
        y_lo = sem("y_lo")
        out_st = sem("out_st")

        def batches(t):
            return t[:, :, :].rearrange("d p (q c) -> d p q c", c=64)[:, :, 0:4:3, :]

        def pairs(K):
            return xs[:, bass.ds(PP * K, PP), :]

        def phase(K, a):
            return K // NG if isinstance(K, int) else a

        def steps(eng, step, first=0):
            step(0, 0, None)
            with eng.Fori(0, 6) as i:
                for c in range(2):
                    step(2 * i + (c + 1), (c + 1) % 2, 0)
            for J in range(13, 17):
                step(J, J % 2, None)
            with eng.Fori(0, 6) as i:
                for c in range(2):
                    step(2 * i + (c + 17), (c + 1) % 2, 1)
            for J in range(29, 32):
                step(J, J % 2, None)

        def known(J):
            return J if isinstance(J, int) else NG // 2

        def prep_plan(a):
            first = (0, 1, 8, 9)
            return ([("T", 4 * q, wT[a][w]) for w in range(3) for q in range(2)]
                    + [("A", n, AW[a]) for n in first] + [("O", n, OW[a]) for n in first])

        def DKW(a, i):
            return (DK[a], D, DK[a])[i // 2]

        def T_BANK(K, i):
            return (i if K == 0 else 8 + 14 + i) % 5

        def prep_bank(a, i):
            return ring[(i if a == 0 else 8 + i) % 5]

        def u_bank(p, c):
            return ring[((2 if p == 0 else 16) + c) % 5]

        def u_src(p, c, a):
            return u_bank(p, c)[0:DK[a], :].rearrange("d (h n) -> d h n", n=N)

        def u_dst(s, p, c, a):
            t = 128 * p + 64 * (c // 2)
            return U[s][0:DK[a], c % 2:H:2, t:t + N]

        block = stack.enter_context(nc.Block())

        @block.sync
        def _(sp):
            xv = x.rearrange("(t b) n d -> (b n) t d", b=2)
            ov = out.rearrange("(t b) n d -> (b n) t d", b=2)

            def load_w(a, w, src):
                if w == 3:
                    sp.dma_start(wo_st[a][:, :, :], src.rearrange("(h p) d -> p h d", p=128)).then_inc(w_in[a][w], 16)
                else:
                    sp.dma_start(wst[a][w][0:src.shape[0], :], src).then_inc(w_in[a][w], 16)

            def load_x(g):
                sp.dma_start(xs[:, PP * g:PP * g + PP, :], xv[:, PP * g:PP * g + PP, :]).then_inc(x_in[g], 16)

            load_w(0, 0, Wk1)
            load_x(0)
            load_w(0, 1, Wq1)
            load_x(1)
            load_w(0, 2, Wv1)
            load_w(0, 3, Wo1)
            load_x(2)
            sp.dma_start(xs[:, 3 * PP:NPAIR, :], xv[:, 3 * PP:NPAIR, :]).then_inc(x_in[3], 16)
            load_w(1, 0, Wk2)
            load_w(1, 1, Wq2)
            load_w(1, 2, Wv2)
            load_w(1, 3, Wo2)
            sp.dma_start(wp_raw[:, :], Wp).then_inc(ff_in, 16)
            sp.dma_start(wf_raw[:, :, :], Wf.rearrange("(c p) d -> p c d", p=128)).then_inc(ff_in, 16)

            def load_context(k, buf, first):
                if not first:
                    sp.wait_ge(kd_ready, 8 * (k + A2 - 1))
                    sp.wait_ge(xt_fill, k + A2 - 1)
                src = ctx_in[bass.ds(GB * k, GB), :, :].rearrange("b s d -> s b d")
                for r in (0, 64):
                    sp.dma_start(cx[buf][r:r + 64, :, :], src).then_inc(cx_in[buf], 16)

            load_context(0, 0, True)
            load_context(1, 1, True)
            with sp.Fori(1, NG // 2) as i:
                for c in range(2):
                    load_context(2 * i + c, c, False)

            def store(f):
                sp.wait_ge(fin_add, f + FFK + 1)
                sp.dma_start(ov[:, bass.ds(PP * f, PP), :], xs[:, bass.ds(PP * f, PP), :]).then_inc(out_st, 16)

            with sp.Fori(0, NG) as f:
                store(f)
            sp.wait_ge(out_st, 16 * NG)

        @block.gpsimd
        def _(pool):
            pool.memset(ident[:, :], 0.0).then_inc(id_done, 1)
            pool.wait_ge(id_done, 1)
            pool.affine_select(out=ident[:, :], in_=ident[:, :], compare_op=ALU.not_equal, fill=1.0,
                               base=0, pattern=[[-1, 128]], channel_multiplier=1).then_inc(id_done, 1)
            pool.memset(neghalf[:, :], -0.5).then_inc(consts, 1)
            pool.memset(epsc[:, :], EPS).then_inc(consts, 1)
            pool.memset(one[:, :], 1.0).then_inc(consts, 1)
            for k in range(2):
                for s in range(2):
                    pool.memset(xt[k][s][:, :, :].bitcast(f32), 0.0).then_inc(consts, 1)
            pool.wait_ge(consts, 3)
            pool.wait_ge(c_in, 160)

            def inverse_std(K):
                pool.wait_ge(ln_var, 2 * K + 2)
                pool.tensor_tensor(veps[:, :], mv[:, :, 1], epsc[:, :], ALU.add).then_inc(eps_done, 1)
                pool.wait_ge(eps_done, K + 1)
                pool.tensor_tensor(rstd[:, :], veps[:, :], neghalf[:, :], ALU.pow).then_inc(ln_rstd, 1)

            def gain_offset(K, ln, first=False):
                pool.wait_ge(ln_z, 2 * K + 2)
                gb = gam[:, ln:ln + 1, :].broadcast_to([128, PP, D])
                bb = bet[:, ln:ln + 1, :].broadcast_to([128, PP, D])
                pool.tensor_tensor(xg[:, :, :], xz[:, :, :], gb, ALU.mult).then_inc(xg_done, 1)
                pool.wait_ge(xg_done, K + 1)
                if not first:
                    pool.wait_ge(xt_fill, K)
                pool.tensor_tensor(xn[:, :, :], xg[:, :, :], bb, ALU.add).then_inc(xn_ready, 1)
                if ln == 0:
                    key_hi(K, ln)

            def key_hi(K, ln):
                pool.tensor_tensor(kn[:, :, :].bitcast(f32r), xg[:, :, :],
                                   bet[:, ln:ln + 1, :].broadcast_to([128, PP, D]), ALU.add).then_inc(kn_hi, 1)

            def key_copies(K, buf, a, first=False):
                if not first and known(K) > 1:
                    pool.wait_ge(u_fill, 8 * K - 8)
                if a == 0:
                    pool.wait_ge(kn_hi, K + 1)
                    pool.wait_ge(xn_ready, K + 1)
                    hi, lo = [t[:, :, :].rearrange("r (p b) d -> r p b d", b=2) for t in kd[buf]]
                    n = 0
                    for b in range(2):
                        rows = slice(64 * b, 64 * b + 64)
                        off = bet[rows, 0:1, :].broadcast_to([64, PP, D])
                        for r in (0, 64):
                            pool.tensor_tensor(hi[r:r + 64, :, b, :], xg[rows, :, :], off, ALU.add)\
                                .then_inc(kd_ready, 1)
                            pool.wait_ge(kd_ready, 8 * K + (n + 1))
                            pool.tensor_tensor(lo[r:r + 64, :, b, :], xn[rows, :, :], kn[rows, :, :],
                                               ALU.subtract).then_inc(kd_ready, 1)
                            pool.wait_ge(kd_ready, 8 * K + (n + 2))
                            n += 2
                else:
                    k = K - A2
                    pool.wait_ge(cx_in[buf], 16 * (k - buf) + 32)
                    pool.tensor_tensor(kd[buf][0][:, :, 0:DC], cx[buf][:, :, :],
                                       one[:, :].unsqueeze(2).broadcast_to([128, GB, DC]), ALU.mult).then_inc(kd_hi, 1)
                    pool.wait_ge(kd_hi, k + 1)
                    pool.tensor_tensor(kd[buf][1][:, :, 0:DC], cx[buf][:, :, :],
                                       kd[buf][0][:, :, 0:DC].bitcast(f32), ALU.subtract).then_inc(kd_ready, 8)

            def normalise(K, p):
                pool.wait_ge(rs_done, 2 * K + p + 1)
                v = P[p][:, :].rearrange("r (h s) -> r h s", h=H)
                pool.tensor_tensor(v, v, rs[:, p, :].unsqueeze(2).broadcast_to([128, H, N]), ALU.mult).then_inc(p_norm, 1)

            def step(J, par, a):
                if known(J) < 31:
                    key_copies(J + 1, 1 - par, phase(J + 1, a))
                gain_offset(J + 2, phase(J + 2, a))
                normalise(J, 1)
                if known(J) < 31:
                    normalise(J + 1, 0)
                inverse_std(J + 3)

            inverse_std(0)
            gain_offset(0, 0, True)
            key_copies(0, 0, 0, True)
            inverse_std(1)
            gain_offset(1, 0)
            normalise(0, 0)
            inverse_std(2)
            steps(pool, step)
            gain_offset(34, 2)
            pool.wait_ge(ff_in, 32)
            pool.wait_ge(s_fill, 4 * FFK)
            pool.wait_ge(o_fill, FFK)
            pool.tensor_copy(wp[0][:, :], wp_raw[:, :]).then_inc(ffw_hi, 1)
            pool.tensor_copy(wf[0][:, :, :], wf_raw[:, :, :]).then_inc(ffw_hi, 1)
            pool.wait_ge(ffw_hi, 2)
            pool.tensor_tensor(wp[1][:, :], wp_raw[:, :], wp[0][:, :].bitcast(f32), ALU.subtract).then_inc(ffw_lo, 1)
            pool.tensor_tensor(wf[1][:, :, :], wf_raw[:, :, :], wf[0][:, :, :].bitcast(f32),
                               ALU.subtract).then_inc(ffw_lo, 1)
            with pool.Fori(35, KEND) as K:
                inverse_std(K)
                gain_offset(K, 2)

        @block.scalar
        def _(act):
            for n, (g, b) in enumerate(((g1, b1), (g2, b2), (g3, b3))):
                act.dma_start(gam[:, n, :], g.partition_broadcast(128)).then_inc(c_in, 16)
                act.dma_start(bet[:, n, :], b.partition_broadcast(128)).then_inc(c_in, 16)
            for n, b in enumerate((bo1, bo2, bf)):
                act.dma_start(bo_col[:, n:n + 1], b.rearrange("(d o) -> d o", o=1)).then_inc(c_in, 16)
            act.dma_start(bp_col[:, :], bp.rearrange("(c p) -> p c", p=128),
                          allow_slow_non_contiguous=True).then_inc(c_in, 16)

            def prepare(a, banks):
                plan = prep_plan(a)
                for i in banks:
                    kind, n, dst = plan[i]
                    m = 14 * a + i
                    bank = prep_bank(a, i)
                    act.wait_ge(prep_fill, m + 1)
                    if kind == "T":
                        act.activation(dst[:, n:n + 2, 0:DKW(a, i)],
                                       bank[:, 0:2 * DKW(a, i)].rearrange("p (h d) -> p h d", h=2),
                                       ACT.Copy).then_inc(prep_a, 1)
                    else:
                        act.activation(dst[0][0:DK[a], n:n + 7:2, :],
                                       bank[0:DK[a], :].rearrange("p (h d) -> p h d", h=4),
                                       ACT.Copy).then_inc(prep_a, 1)

            def xt_half(K, par, a, first=False):
                act.wait_ge(xt_fill, K + 1)
                if not first:
                    act.wait_ge(s_fill, 4 * K - 4)
                act.activation(batches(xt[par][0]), ps_m[:, 0:GT].rearrange("d (p q c) -> d p q c", q=2, c=64),
                               ACT.Copy).then_inc(xt_hi, 1)
                if a == 1:
                    act.wait_ge(t_fill, 8 * K)
                    act.activation(ct[0][0:DC, :], ps_m[0:DC, GT:2 * GT], ACT.Copy).then_inc(ct_hi, 1)

            def t_half(K, a, first=False, banks=range(TF)):
                for i in banks:
                    act.wait_ge(t_fill, 8 * K + (i + 1))
                    if not first and i == 0:
                        act.wait_ge(s_fill, 4 * K)
                    bank = T_BANK(K, i) if first == 1 or first == 2 else (8 + i) % 5
                    act.activation(T[0][:, :, 2 * i:2 * i + 2, :].rearrange("d b h s -> d h b s"),
                                   ring[bank][:, :].rearrange("d (h b s) -> d h b s", h=2, b=GB),
                                   ACT.Copy).then_inc(t_hi, 1)

            def exps(K, p, halves=(0, 1)):
                for h in halves:
                    act.wait_ge(s_sub, 4 * K + (2 * p + h + 1))
                    v = P[p][:, HALF * h:HALF * h + HALF]
                    act.activation(v, v, ACT.Exp, scale=SCALE).then_inc(exp_done, 1)

            def pt_half(K, p, first=False):
                for q in range(2):
                    act.wait_ge(pt_fill, 4 * K + (2 * p + q + 1))
                    if q == 0 and not (first and p == 0):
                        act.wait_ge(u_fill, 8 * K + 4 * p)
                    act.activation(pt[0][:, 4 * q:4 * q + 4, :],
                                   ring[(6 * p + q) % 5][:, :].rearrange("r (h c) -> r h c", h=4),
                                   ACT.Copy).then_inc(pt_hi, 1)

            def u_half(K, p, a, first=False):
                for c in range(4):
                    act.wait_ge(u_fill, 8 * K + (4 * p + c + 1))
                    if c == 0 and p == 0 and not first:
                        act.wait_ge(o_fill, K)
                    act.activation(u_dst(0, p, c, a), u_src(p, c, a), ACT.Copy).then_inc(u_hi, 1)

            def out_copy(K, a, src):
                act.wait_ge(o_fill, K + 1)
                if not (isinstance(K, int) and K == 0):
                    act.wait_ge(fin_fill, K)
                act.activation(oT[:, :], src, ACT.Identity, bias=bo_col[:, a:a + 1]).then_inc(o_out, 1)

            def step(J, par, a):
                pt_half(J, 0, known(J) == 0)
                if known(J) < 31:
                    exps(J + 1, 0)
                if known(J) > 0:
                    out_copy(J - 1, phase(J - 1, a), ps_m[:, 0:GT])
                u_half(J, 0, phase(J, a), known(J) == 0)
                pt_half(J, 1)
                xt_half(J + 2, par, phase(J + 2, a))
                if known(J) < 31:
                    exps(J + 1, 1, (0,))
                if known(J) < 30:
                    t_half(J + 2, phase(J + 2, a), banks=range(2))
                if known(J) < 31:
                    exps(J + 1, 1, (1,))
                if known(J) < 30:
                    t_half(J + 2, phase(J + 2, a), banks=range(2, TF))
                u_half(J, 1, phase(J, a))

            prepare(0, range(14))
            act.wait_ge(c_in, 160)
            act.wait_ge(consts, 7)
            xt_half(0, 0, 0, True)
            t_half(0, 0, 1)
            xt_half(1, 1, 0, True)
            exps(0, 0)
            prepare(1, range(6))
            exps(0, 1)
            prepare(1, range(6, 14))
            t_half(1, 0, 2)
            steps(act, step)
            out_copy(31, 1, ps_m[:, 0:GT])

            def ff_xt(K, par):
                act.wait_ge(xt_fill, K + 1)
                act.activation(batches(xt[par][0]), ring[2][:, 0:GT].rearrange("d (p q c) -> d p q c", q=2, c=64),
                               ACT.Copy).then_inc(xt_hi, 1)

            def gelus(f, first=False):
                for c in range(NCH):
                    act.wait_ge(gate_fill, 2 * f + (c // 2 + 1))
                    if not first:
                        act.wait_ge(y_done, 4 * f - (3 - c))
                    act.activation(gel[:, c, :], ps_s[c // 2][:, GT * (c % 2):GT * (c % 2) + GT], ACT.Gelu,
                                   bias=bp_col[:, NCH + c:NCH + c + 1]).then_inc(gel_done, 1)

            def y_half(f):
                act.wait_ge(y_done, 4 * f + 4)
                act.wait_ge(o_fill, f + FFK)
                act.activation(yh[0][:, :, :], yf[:, :, :], ACT.Copy).then_inc(y_hi, 1)

            def ff_step(f, par, first=False, turn=True, up=True):
                if up:
                    gelus(f, first)
                if turn:
                    ff_xt(f + (FFK + 2), par)
                if up:
                    y_half(f)
                if not first:
                    out_copy(f + (FFK - 1), 2, ring[3][:, 0:GT])

            ff_step(0, 0, True)
            ff_step(1, 1)
            with act.Fori(0, 6) as i:
                for c in range(2):
                    ff_step(2 * i + (c + 2), c)
            ff_step(14, 0, turn=False)
            ff_step(15, 1, turn=False)
            ff_step(16, 0, turn=False, up=False)

        @block.vector
        def _(dve):
            def prepare(a, banks):
                plan = prep_plan(a)
                for i in banks:
                    kind, n, dst = plan[i]
                    m = 14 * a + i
                    bank = prep_bank(a, i)
                    dve.wait_ge(prep_a, m + 1)
                    if kind == "T":
                        w = DKW(a, i)
                        dve.tensor_copy(dst[:, n + 2:n + 4, 0:w],
                                        bank[:, 2 * w:4 * w].rearrange("p (h d) -> p h d", h=2))\
                            .then_inc(prep_v, 1)
                    else:
                        dve.tensor_tensor(dst[1][0:DK[a], n:n + 7:2, :],
                                          bank[0:DK[a], :].rearrange("p (h d) -> p h d", h=4),
                                          dst[0][0:DK[a], n:n + 7:2, :].bitcast(f32), ALU.subtract)\
                            .then_inc(prep_v, 1)

            def xrow(K, a, p):
                return xs[:, bass.ds(PP * (K - a * NG) + p, 1), :].rearrange("r o d -> r (o d)")

            def norm_stats(K, a, first=False):
                if a > 0:
                    dve.wait_ge(fin_add, K - (NG - 1))
                for p in range(PP):
                    dve.bn_stats(stats[:, p, :], xrow(K, a, p)).then_inc(st_done, 1)

            def norm_aggregate(K):
                for p in range(PP):
                    dve.bn_aggr(mv[:, p, :], stats[:, p, :]).then_inc(ln_var, 1)

            def norm_apply(K, a, first=False):
                dve.wait_ge(ln_rstd, K + 1)
                if not first:
                    dve.wait_ge(xg_done, K)
                for p in range(PP):
                    dve.tensor_scalar(xz[:, p, :], xrow(K, a, p), mv[:, p, 0:1], rstd[:, p:p + 1],
                                      ALU.subtract, ALU.mult).then_inc(ln_z, 1)

            def xt_rest(K, par, a, src):
                dve.wait_ge(xt_hi, K + 1)
                if a == 1:
                    dve.wait_ge(ct_hi, K - (A2 - 1))
                dve.tensor_tensor(batches(xt[par][1]), src[:, 0:GT].rearrange("d (p q c) -> d p q c", q=2, c=64),
                                  batches(xt[par][0]).bitcast(f32),
                                  ALU.subtract).then_inc(xt_lo, 1)
                if a == 1:
                    dve.tensor_tensor(ct[1][0:DC, :], ps_m[0:DC, GT:2 * GT], ct[0][0:DC, :].bitcast(f32),
                                      ALU.subtract).then_inc(ct_lo, 1)

            def t_rest(K, first=0):
                for i in range(TF):
                    dve.wait_ge(t_hi, 8 * K + (i + 1))
                    bank = T_BANK(K, i) if first else (8 + i) % 5
                    dst = [t[:, :, 2 * i:2 * i + 2, :].rearrange("d b h s -> d h b s") for t in T]
                    dve.tensor_tensor(dst[1], ring[bank][:, :].rearrange("d (h b s) -> d h b s", h=2, b=GB),
                                      dst[0].bitcast(f32), ALU.subtract).then_inc(t_lo, 1)

            def maxes(K, p, first=False):
                for h in range(2):
                    dve.wait_ge(s_fill, 4 * K + (2 * p + h + 1))
                    v = ps_s[h][:, :].rearrange("r (h s) -> r h s", s=N)
                    m = mx[:, p, HP * h:HP * h + HP]
                    dve.tensor_reduce(m, v, AX.X, ALU.max).then_inc(mx_done, 1)
                    dve.wait_ge(mx_done, 4 * K + (2 * p + h + 1))
                    if not first:
                        dve.wait_ge(pt_fill, 4 * K + (2 * p - 2))
                    dve.tensor_tensor(P[p][:, HALF * h:HALF * h + HALF].rearrange("r (h s) -> r h s", s=N), v,
                                      m.unsqueeze(2).broadcast_to([128, HP, N]), ALU.subtract).then_inc(s_sub, 1)

            def sums(K, p):
                dve.wait_ge(exp_done, 4 * K + (2 * p + 2))
                dve.tensor_reduce(sm[:, p, :], P[p][:, :].rearrange("r (h s) -> r h s", s=N), AX.X,
                                  ALU.add).then_inc(sum_done, 1)
                dve.wait_ge(sum_done, 2 * K + (p + 1))
                dve.reciprocal(rs[:, p, :], sm[:, p, :]).then_inc(rs_done, 1)

            def pt_rest(K, p):
                for q in range(2):
                    dve.wait_ge(pt_hi, 4 * K + (2 * p + q + 1))
                    dve.tensor_tensor(pt[1][:, 4 * q:4 * q + 4, :],
                                      ring[(6 * p + q) % 5][:, :].rearrange("r (h c) -> r h c", h=4),
                                      pt[0][:, 4 * q:4 * q + 4, :].bitcast(f32), ALU.subtract).then_inc(pt_lo, 1)

            def u_rest(K, p, a, banks=range(4)):
                for c in banks:
                    dve.wait_ge(u_hi, 8 * K + (4 * p + c + 1))
                    dve.tensor_tensor(u_dst(1, p, c, a), u_src(p, c, a), u_dst(0, p, c, a).bitcast(f32),
                                      ALU.subtract).then_inc(u_lo, 1)

            def fin(K, a, src):
                dve.wait_ge(fin_fill, K + 1)
                v = pairs(K - a * NG)
                dve.tensor_tensor(v, src[:, 0:GT].rearrange("r (p d) -> r p d", p=PP), v, ALU.add)\
                    .then_inc(fin_add, 1)

            def step(J, par, a):
                pt_rest(J, 0)
                if known(J) < 31:
                    maxes(J + 1, 0)
                sums(J, 1)
                norm_stats(J + 3, phase(J + 3, a))
                dve.wait_ge(st_done, 2 * J + 8)
                if known(J) < 31:
                    sums(J + 1, 0)
                u_rest(J, 0, phase(J, a), range(2))
                norm_aggregate(J + 3)
                if known(J) > 0:
                    fin(J - 1, phase(J - 1, a), ps_m)
                u_rest(J, 0, phase(J, a), range(2, 4))
                pt_rest(J, 1)
                xt_rest(J + 2, par, phase(J + 2, a), ps_m)
                if known(J) < 31:
                    maxes(J + 1, 1)
                if known(J) < 30:
                    t_rest(J + 2)
                norm_apply(J + 3, phase(J + 3, a))
                u_rest(J, 1, phase(J, a))

            def norm_first(g):
                dve.wait_ge(x_in[g], 16)
                norm_stats(g, 0)
                dve.wait_ge(st_done, 2 * g + 2)
                norm_aggregate(g)

            norm_first(0)
            prepare(0, range(1))
            norm_apply(0, 0, True)
            norm_first(1)
            prepare(0, range(1, 6))
            norm_apply(1, 0)
            prepare(0, range(6, 14))
            xt_rest(0, 0, 0, ps_m)
            t_rest(0, 1)
            xt_rest(1, 1, 0, ps_m)
            maxes(0, 0, True)
            maxes(0, 1, True)
            prepare(1, range(6))
            sums(0, 0)
            norm_first(2)
            prepare(1, range(6, 14))
            norm_apply(2, 0)
            t_rest(1, 1)
            dve.wait_ge(x_in[3], 16)
            steps(dve, step)
            fin(31, 1, ps_m)

            def products(f, first=False):
                for c in range(NCH):
                    dve.wait_ge(gel_done, 4 * f + (c + 1))
                    dve.wait_ge(a_fill, 2 * f + (c // 2 + 1))
                    if not first and c == 0:
                        dve.wait_ge(y_hi, f)
                        dve.wait_ge(y_lo, f)
                    dve.scalar_tensor_tensor(yf[:, c, :], ring[c // 2][:, GT * (c % 2):GT * (c % 2) + GT],
                                             bp_col[:, c:c + 1], gel[:, c, :], ALU.add, ALU.mult)\
                        .then_inc(y_done, 1)

            def y_rest(f):
                dve.wait_ge(y_hi, f + 1)
                dve.tensor_tensor(yh[1][:, :, :], yf[:, :, :], yh[0][:, :, :].bitcast(f32),
                                  ALU.subtract).then_inc(y_lo, 1)

            def ff_step(f, par, first=False, turn=True, stat=True, up=True, finish=True):
                if up:
                    products(f, first)
                if stat:
                    norm_stats(f + (FFK + 3), 2)
                    dve.wait_ge(st_done, 2 * f + (2 * FFK + 8))
                if turn:
                    xt_rest(f + (FFK + 2), par, 2, ring[2])
                if finish:
                    fin(f + (FFK - 2), 2, ring[4])
                if stat:
                    norm_aggregate(f + (FFK + 3))
                if up:
                    y_rest(f)
                if stat:
                    norm_apply(f + (FFK + 3), 2)

            ff_step(0, 0, True, finish=False)
            ff_step(1, 1, finish=False)
            with dve.Fori(0, 5) as i:
                for c in range(2):
                    ff_step(2 * i + (c + 2), c)
            ff_step(12, 0)
            ff_step(13, 1, stat=False)
            ff_step(14, 0, turn=False, stat=False)
            ff_step(15, 1, turn=False, stat=False)
            ff_step(16, 0, turn=False, stat=False, up=False)
            ff_step(17, 1, turn=False, stat=False, up=False)

        @block.tensor
        def _(pe):
            def prepare(a):
                for i, (kind, n, dst) in enumerate(prep_plan(a)):
                    m = 14 * a + i
                    if i >= 5:
                        pe.wait_ge(prep_v, m - 4)
                    bank = prep_bank(a, i)
                    if kind == "T":
                        w = i // 2
                        pe.wait_ge(w_in[a][w], 16)
                        d = DKW(a, i)
                        for j in range(4):
                            last = pe.transpose(bank[:, d * j:d * j + d],
                                                wst[a][w][0:d, 128 * (n + j):128 * (n + j) + 128],
                                                ident[0:d, 0:d])
                    else:
                        if i == 6:
                            pe.wait_ge(prep_v, 14 * a + 4)
                        if i == 10:
                            pe.wait_ge(prep_v, 14 * a + 6)
                            pe.wait_ge(w_in[a][3], 16)
                        left = wT[a][0 if kind == "A" else 2]
                        right = wT[a][1] if kind == "A" else wo_st[a]
                        for j in range(4):
                            hp, r = (n + 2 * j) // 2, 64 * (n % 2)
                            last = pe.matmul(bank[0:DK[a], 128 * j:128 * j + 128], left[r:r + 64, hp, 0:DK[a]],
                                             right[r:r + 64, hp, :], start=True, stop=True)
                    last.then_inc(prep_fill, 1)

            def turn(K, par, a, bank, first=False):
                if a == 1:
                    k = K - A2
                    pe.wait_ge(cx_in[par], 16 * (k - par) + 32)
                pe.wait_ge(xn_ready, K + 1)
                if first:
                    if K > 0:
                        pe.wait_ge(xt_lo, K)
                else:
                    pe.wait_ge(fin_add, K - 2)
                for p in range(PP):
                    last = pe.transpose(bank[:, 128 * p:128 * p + 128], xn[:, p, :], ident[:, :])
                if a == 1:
                    for b in range(GB):
                        last = pe.transpose(bank[0:DC, GT + N * b:GT + N * b + N], cx[par][0:64, b, :],
                                            ident[0:64, 0:64])
                last.then_inc(xt_fill, 1)

            def t_products(K, par, a, first=0):
                pe.wait_ge(xt_lo, K + 1)
                if a == 1:
                    pe.wait_ge(ct_lo, K - (A2 - 1))
                mov = [batches(t) for t in xt[par]] if a == 0 else [t[0:DC, :] for t in ct]
                for i in range(TF):
                    if first:
                        bank = T_BANK(K, i)
                        if i >= 5:
                            pe.wait_ge(t_lo, 8 * K + i - 4)
                        elif K == 1:
                            pe.wait_ge(prep_v, 24 + i)
                    else:
                        bank = (8 + i) % 5
                        if i < 3:
                            pe.wait_ge(u_lo, 8 * (K - 2) + (i + 2))
                        elif i < 5:
                            pe.wait_ge(pt_lo, 4 * (K - 2) + i)
                        else:
                            pe.wait_ge(t_lo, 8 * K + (i - 4))
                    for j in range(2):
                        o = ring[bank][:, GT * j:GT * j + GT]
                        for n, (s, m) in enumerate(PARTS):
                            last = pe.matmul(o, AW[a][s][0:DK[a], 2 * i + j, :], mov[m],
                                             start=(n == 0), stop=(n == 2))
                    last.then_inc(t_fill, 1)

            def scores(K, p, par, first=False):
                if p == 0:
                    pe.wait_ge(t_lo, 8 * K + 8)
                for h in range(2):
                    if not (first and p == 0):
                        pe.wait_ge(s_sub, 4 * K + (2 * p + h - 1))
                    n = 0
                    for b in range(2):
                        for s, m in PARTS:
                            last = pe.matmul(ps_s[h][:, :], xt[par][s][:, p, 128 * b:128 * b + 128],
                                             T[m][:, 2 * p + b, 8 * h:8 * h + 8, :].rearrange("d h s -> d (h s)"),
                                             start=(n == 0), stop=(n == 5))
                            n += 1
                    last.then_inc(s_fill, 1)

            def turn_softmax(K, p, with_t=True):
                pe.wait_ge(p_norm, 2 * K + (p + 1))
                if p == 0 and with_t:
                    pe.wait_ge(t_lo, 8 * K + 16)
                for q in range(2):
                    if p == 1 and q == 1:
                        pe.wait_ge(u_lo, 8 * K + 1)
                    if p == 0 and q == 1 and known(K) > 0:
                        pe.wait_ge(u_lo, 8 * K - 3)
                    for j in range(4):
                        hp = 4 * q + j
                        last = pe.transpose(ring[(6 * p + q) % 5][:, 128 * j:128 * j + 128],
                                            P[p][:, 128 * hp:128 * hp + 128], ident[:, :])
                    last.then_inc(pt_fill, 1)

            def u_products(K, p, par, a, with_t=True, banks=range(4)):
                pe.wait_ge(pt_lo, 4 * K + (2 * p + 2))
                pe.wait_ge(kd_ready, 8 * K + 8)
                for c in banks:
                    b, r = c // 2, 64 * (c % 2)
                    if p == 1:
                        if with_t:
                            pe.wait_ge(t_lo, 8 * (K + 2) + (c + 4))
                        elif c == 0:
                            pe.wait_ge(u_lo, 8 * K + 4)
                    for n, (s, m) in enumerate(PARTS):
                        last = pe.matmul(u_src(p, c, a).rearrange("d h n -> d (h n)"),
                                         kd[par][s][r:r + 64, 2 * p + b, 0:DK[a]],
                                         pt[m][r:r + 64, :, 64 * b:64 * b + 64], start=(n == 0), stop=(n == 2))
                    last.then_inc(u_fill, 1)

            def out_products(K, a, turned=True):
                pe.wait_ge(u_lo, 8 * K + 8)
                pe.wait_ge(xt_lo, K + 3)
                if turned == 1:
                    pe.wait_ge(ct_lo, K - (A2 - 3))
                n = 0
                for h in range(H):
                    for s, m in PARTS:
                        last = pe.matmul(ps_m[:, 0:GT], OW[a][s][0:DK[a], h, :], U[m][0:DK[a], h, :],
                                         start=(n == 0), stop=(n == 3 * H - 1))
                        n += 1
                last.then_inc(o_fill, 1)

            def turn_back(K, bank):
                pe.wait_ge(o_out, K + 1)
                for p in range(PP):
                    last = pe.transpose(bank[:, 128 * p:128 * p + 128], oT[:, 128 * p:128 * p + 128], ident[:, :])
                last.then_inc(fin_fill, 1)

            def step(J, par, a):
                turn_softmax(J, 0, known(J) < 31)
                if known(J) < 31:
                    scores(J + 1, 0, 1 - par)
                if known(J) > 0:
                    out_products(J - 1, phase(J - 1, a), phase(J + 1, a))
                u_products(J, 0, par, phase(J, a), banks=range(2))
                if known(J) > 0:
                    turn_back(J - 1, ps_m)
                u_products(J, 0, par, phase(J, a), banks=range(2, 4))
                turn_softmax(J, 1)
                turn(J + 2, par, phase(J + 2, a), ps_m, known(J) == 0)
                if known(J) < 31:
                    scores(J + 1, 1, 1 - par)
                if known(J) < 30:
                    t_products(J + 2, par, phase(J + 2, a))
                u_products(J, 1, par, phase(J, a), known(J) < 30)

            pe.wait_ge(id_done, 2)
            prepare(0)
            pe.wait_ge(prep_v, 14)
            turn(0, 0, 0, ps_m, True)
            t_products(0, 0, 0, 1)
            turn(1, 1, 0, ps_m, True)
            scores(0, 0, 0, True)
            scores(0, 1, 0)
            prepare(1)
            t_products(1, 1, 0, 1)
            steps(pe, step)
            out_products(31, 1, 2)
            turn_back(31, ps_m)

            def up_products(f, par, first=False):
                K = f + FFK
                pe.wait_ge(xt_lo, K + 1)
                mov = [batches(t) for t in xt[par]]
                for c in range(2 * NCH):
                    gate = c < NCH
                    i, j = (c % NCH) // 2, c % 2
                    if not first and j == 0:
                        if gate:
                            pe.wait_ge(gel_done, 4 * f - (2 - 2 * i))
                        else:
                            pe.wait_ge(y_done, 4 * f - (2 - 2 * i))
                    o = (ps_s if gate else ring)[i][:, GT * j:GT * j + GT]
                    col = 128 * (c % NCH) + (FF if gate else 0)
                    for n, (s, m) in enumerate(PARTS):
                        last = pe.matmul(o, wp[s][:, col:col + 128], mov[m], start=(n == 0), stop=(n == 2))
                    if j == 1:
                        last.then_inc(gate_fill if gate else a_fill, 1)

            def down_products(f):
                K = f + FFK
                pe.wait_ge(y_lo, f + 1)
                pe.wait_ge(o_out, K)
                n = 0
                for c in range(NCH):
                    for s, m in PARTS:
                        last = pe.matmul(ring[3][:, 0:GT], wf[s][:, c, :], yh[m][:, c, :],
                                         start=(n == 0), stop=(n == 3 * NCH - 1))
                        n += 1
                last.then_inc(o_fill, 1)

            def ff_turn(K):
                pe.wait_ge(xn_ready, K + 1)
                pe.wait_ge(xt_lo, K)
                for p in range(PP):
                    last = pe.transpose(ring[2][:, 128 * p:128 * p + 128], xn[:, p, :], ident[:, :])
                last.then_inc(xt_fill, 1)

            def ff_step(f, par, first=False, up=True, down=True, back=True, norm=True):
                if up:
                    up_products(f, par, first)
                if norm:
                    ff_turn(f + (FFK + 2))
                if back:
                    K = f + (FFK - 2)
                    pe.wait_ge(fin_add, K)
                    turn_back(K, ring[4])
                if down:
                    down_products(f - 1)

            pe.wait_ge(ffw_lo, 2)
            ff_step(0, 0, True, down=False, back=False)
            ff_step(1, 1, back=False)
            with pe.Fori(0, 6) as i:
                for c in range(2):
                    ff_step(2 * i + (c + 2), c)
            ff_step(14, 0, norm=False)
            ff_step(15, 1, norm=False)
            ff_step(16, 0, norm=False, up=False)
            ff_step(17, 1, norm=False, up=False, down=False)


_INS = ["x", "ctx_768"] + [f"L0_xattn_{n}" for n in
        ("Wq1", "Wk1", "Wv1", "Wo1", "bo1", "Wq2", "Wk2", "Wv2", "Wo2", "bo2", "Wp", "bp", "Wf", "bf",
         "g1", "b1", "g2", "b2", "g3", "b3")]


def kernel(**inputs):
    import numpy as _np
    import concourse.bacc as _bacc
    from concourse import mybir as _mybir
    from concourse.bass_utils import run_bass_kernel_spmd as _run

    nc = _bacc.Bacc("TRN2", target_bir_lowering=False, num_devices=1)
    arrays, args = {}, []
    for name in _INS:
        a = _np.ascontiguousarray(inputs[name])
        arrays[f"in_{name}"] = a
        args.append(nc.dram_tensor(f"in_{name}", a.shape, _mybir.dt.from_np(a.dtype), kind="ExternalInput").ap())
    o = nc.dram_tensor("out", arrays["in_x"].shape, _mybir.dt.from_np(arrays["in_x"].dtype),
                       kind="ExternalOutput").ap()
    xattn_block(nc, *args, o)
    r = _run(nc, [arrays], core_ids=[0])
    return r.results[0]["out"]
```

```python
import concourse.bass as bass
from concourse import mybir
from concourse.alu_op_type import AluOpType as ALU
from contextlib import ExitStack


def xattn_block(nc, x, ctx_in, Wq1, Wk1, Wv1, Wo1, bo1, Wq2, Wk2, Wv2, Wo2, bo2, Wp, bp, Wf, bf,
                g1, b1, g2, b2, g3, b3, out):
    f32 = mybir.dt.float32
    f32r = mybir.dt.float32r
    ACT = mybir.ActivationFunctionType
    AX = mybir.AxisListType

    B, N, D = x.shape
    DC = ctx_in.shape[2]
    INNER = Wq1.shape[1]
    DH = 64
    H = INNER // DH
    HP = H // 2
    FF = Wf.shape[0]
    GB = 4
    PP = GB // 2
    GT = GB * N
    NG = B // GB
    NPAIR = B // 2
    SCALE = DH ** -0.5
    EPS = 1e-5
    HALF = H // 2 * N
    TF = H * GT // 512
    NCH = FF // 128
    PARTS = ((0, 0), (1, 0), (0, 1))
    DK = (D, DC)
    A2, FFK = NG, 2 * NG
    OUT_SPLIT = (range(8), range(8, 11), range(11, H))

    stack = ExitStack()
    with stack:
        def sb(name, shape, dt=f32):
            return stack.enter_context(nc.sbuf_tensor(name, shape, dt))

        def sem(name):
            return stack.enter_context(nc.semaphore(name))

        xs = sb("xs", [128, NPAIR, D])
        ident = sb("ident", [128, 128])
        AW = [[sb(f"AW{a}{s}", [128, H, D], f32r) for s in "hl"] for a in range(2)]
        OW = [[sb(f"OW{a}{s}", [128, H, D], f32r) for s in "hl"] for a in range(2)]
        wp_raw = sb("wp_raw", [128, 2 * FF])
        wf_raw = sb("wf_raw", [128, NCH, D])
        gam = sb("gam", [128, 3, D])
        bet = sb("bet", [128, 3, D])
        bo_col = sb("bo_col", [128, 3])
        bp_col = sb("bp_col", [128, 2 * NCH])
        xt = [[sb(f"xt{k}{s}", [128, PP, 4 * 64], f32r) for s in "hl"] for k in range(2)]
        kd = [[sb(f"kd{k}{s}", [128, GB, 128], f32r) for s in "hl"] for k in range(2)]
        kn = sb("kn", [128, PP, D])
        cx = [sb(f"cx{k}", [128, GB, DC]) for k in range(2)]
        ct = [sb(f"ct{s}", [128, GT], f32r) for s in "hl"]
        P0 = sb("P0", [128, H * N])
        P1 = [sb(f"P1{k}", [128, H * N]) for k in range(2)]
        pt = sb("pt", [128, HP, 2, 128], f32r)
        xz = sb("xz", [128, PP, D])
        xg = sb("xg", [128, PP, D])
        xn = sb("xn", [128, PP, D])
        oT = sb("oT", [128, GT])
        stats = sb("stats", [128, PP, 6])
        mv = sb("mv", [128, PP, 2])
        veps = sb("veps", [128, PP])
        rstd = sb("rstd", [128, PP])
        neghalf = sb("neghalf", [128, PP])
        epsc = sb("epsc", [128, PP])
        one = sb("one", [128, 1])
        mx = sb("mx", [128, PP, H])
        nmx = sb("nmx", [128, H])
        sm = sb("sm", [128, PP, H])
        rs = sb("rs", [128, PP, H])
        fold = [sb(f"fold{n}", [128, H, n]) for n in (32, 16, 8)]

        with ExitStack() as region:
            def rb(name, shape, dt=f32):
                return region.enter_context(nc.sbuf_tensor(name, shape, dt))
            wst, wT, wo_st = [], [], []
            for a in range(2):
                wst.append([rb(f"wst{a}{w}", [128, INNER]) for w in "kqv"])
                wT.append([rb(f"wT{a}{w}", [128, HP, 128]) for w in "kq"])
                if a == 1:
                    wo_st.append(rb("wo_st1", [128, HP, D]))
                    wT[1].append(rb("wT1v", [128, HP, 128]))
                else:
                    wo_st.append(P0[:, :].rearrange("p (h d) -> p h d", h=HP))
                    wT[0].append(P1[0][:, :].rearrange("p (h d) -> p h d", h=HP))
                    rb("spare", [128, 2 * GB * H * N - 5 * INNER])
        with ExitStack() as region:
            T = [rb(f"T{s}", [128, GB, H, N], f32r) for s in "hl"]
            U = [rb(f"U{s}", [128, H, GT], f32r) for s in "hl"]
        with ExitStack() as region:
            wp = [rb(f"wp{s}", [128, 2 * FF], f32r) for s in "hl"]
            wf = [rb(f"wf{s}", [128, NCH, D], f32r) for s in "hl"]
            gel = rb("gel", [128, NCH, GT])
            yf = [rb(f"yf{k}", [128, NCH, GT]) for k in range(2)]
            yh = [[rb(f"y{k}{s}", [128, NCH, GT], f32r) for s in "hl"] for k in range(2)]

        ps_s = [stack.enter_context(nc.psum_tensor(f"ps_s{i}", [128, 512], f32)) for i in range(2)]
        ring = [stack.enter_context(nc.psum_tensor(f"ring{i}", [128, 512], f32)) for i in range(5)]
        ps_m = stack.enter_context(nc.psum_tensor("ps_m", [128, 512], f32))

        w_in = [[sem(f"w_in{a}{w}") for w in "kqvo"] for a in range(2)]
        x_in = [sem(f"x_in{i}") for i in range(4)]
        g_in = sem("g_in")
        c_in = sem("c_in")
        ff_in = sem("ff_in")
        cx_in = [sem(f"cx_in{k}") for k in range(2)]
        id_done = sem("id_done")
        consts = sem("consts")
        prep_fill = sem("prep_fill")
        prep_a = sem("prep_a")
        prep_v = sem("prep_v")
        st_done = sem("st_done")
        ln_var = sem("ln_var")
        eps_done = sem("eps_done")
        ln_rstd = sem("ln_rstd")
        ln_c = sem("ln_c")
        ln_z = sem("ln_z")
        xg_done = sem("xg_done")
        xn_ready = sem("xn_ready")
        kn_hi = sem("kn_hi")
        kd_hi = sem("kd_hi")
        kd_ready = sem("kd_ready")
        xt_fill = sem("xt_fill")
        xt_hi = sem("xt_hi")
        xt_lo = sem("xt_lo")
        ct_hi = sem("ct_hi")
        ct_lo = sem("ct_lo")
        t_fill = sem("t_fill")
        t_hi = sem("t_hi")
        t_lo = sem("t_lo")
        s_fill = sem("s_fill")
        mx_done = sem("mx_done")
        nmx_done = sem("nmx_done")
        s_sub = sem("s_sub")
        exp_0 = sem("exp_0")
        exp_1 = sem("exp_1")
        fold_done = sem("fold_done")
        sum_done = sem("sum_done")
        rs_done = sem("rs_done")
        p_norm = sem("p_norm")
        pt_fill = sem("pt_fill")
        pt_hi = sem("pt_hi")
        pt_lo = sem("pt_lo")
        u_fill = sem("u_fill")
        u_hi = sem("u_hi")
        u_lo = sem("u_lo")
        o_fill = sem("o_fill")
        o_out = sem("o_out")
        fin_fill = sem("fin_fill")
        fin_add = sem("fin_add")
        ffw_hi = sem("ffw_hi")
        ffw_lo = sem("ffw_lo")
        gate_fill = sem("gate_fill")
        gel_done = sem("gel_done")
        a_fill = sem("a_fill")
        y_done = sem("y_done")
        y_hi = sem("y_hi")
        y_lo = sem("y_lo")
        y_lo_2 = sem("y_lo_2")
        out_st = sem("out_st")

        def batches(t):
            return t[:, :, :].rearrange("d p (q c) -> d p q c", c=64)[:, :, 0:4:3, :]

        def pairs(K):
            return xs[:, bass.ds(PP * K, PP), :]

        def phase(K, a):
            return K // NG if isinstance(K, int) else a

        def steps(eng, step, before_last=None):
            step(0, 0, None)
            with eng.Fori(0, 6) as i:
                for c in range(2):
                    step(2 * i + (c + 1), (c + 1) % 2, 0)
            for J in range(13, 17):
                step(J, J % 2, None)
            with eng.Fori(0, 6) as i:
                for c in range(2):
                    step(2 * i + (c + 17), (c + 1) % 2, 1)
            step(29, 1, None)
            step(30, 0, None)
            if before_last:
                before_last()
            step(31, 1, None)

        def known(J):
            return J if isinstance(J, int) else NG // 2

        def prep_plan(a):
            first = (0, 1, 8, 9)
            return ([("T", 4 * q, wT[a][w]) for w in range(3) for q in range(2)]
                    + [("A", n, AW[a]) for n in first] + [("O", n, OW[a]) for n in first])

        def DKW(a, i):
            return (DK[a], D, DK[a])[i // 2]

        def first_t_bank(K, i):
            return (10 + i if K == 0 else 36 + i) % 5

        def prep_bank(m):
            return ring[(m if m < 10 else 8 + m) % 5]

        def u_bank(p, c):
            return ring[((2 if p == 0 else 16) + c) % 5]

        def u_src(p, c, a):
            return u_bank(p, c)[0:DK[a], :].rearrange("d (h n) -> d h n", n=N)

        def u_dst(s, p, c, a):
            t = 128 * p + 64 * (c // 2)
            return U[s][0:DK[a], c % 2:H:2, t:t + N]

        block = stack.enter_context(nc.Block())

        @block.sync
        def _(sp):
            xv = x.rearrange("(t b) n d -> (b n) t d", b=2)
            ov = out.rearrange("(t b) n d -> (b n) t d", b=2)

            def load_w(a, w, src):
                if w == 3:
                    sp.dma_start(wo_st[a][:, :, :], src.rearrange("(h p) d -> p h d", p=128)).then_inc(w_in[a][w], 16)
                else:
                    sp.dma_start(wst[a][w][0:src.shape[0], :], src).then_inc(w_in[a][w], 16)

            def load_x(g):
                sp.dma_start(xs[:, PP * g:PP * g + PP, :], xv[:, PP * g:PP * g + PP, :]).then_inc(x_in[g], 16)

            def load_norm(n, g, b, done):
                sp.dma_start(gam[:, n, :], g.partition_broadcast(128)).then_inc(done, 16)
                sp.dma_start(bet[:, n, :], b.partition_broadcast(128)).then_inc(done, 16)

            load_w(0, 0, Wk1)
            load_w(0, 1, Wq1)
            load_x(0)
            load_norm(0, g1, b1, g_in)
            load_x(1)
            load_w(0, 2, Wv1)
            load_w(0, 3, Wo1)
            load_x(2)
            sp.dma_start(xs[:, 3 * PP:NPAIR, :], xv[:, 3 * PP:NPAIR, :]).then_inc(x_in[3], 16)
            load_w(1, 0, Wk2)
            load_w(1, 1, Wq2)
            load_w(1, 2, Wv2)
            load_w(1, 3, Wo2)
            load_norm(1, g2, b2, c_in)
            load_norm(2, g3, b3, c_in)
            for n, b in enumerate((bo1, bo2, bf)):
                sp.dma_start(bo_col[:, n:n + 1], b.rearrange("(d o) -> d o", o=1)).then_inc(c_in, 16)
            sp.dma_start(bp_col[:, :], bp.rearrange("(c p) -> p c", p=128),
                         allow_slow_non_contiguous=True).then_inc(c_in, 16)
            sp.dma_start(wp_raw[:, :], Wp).then_inc(ff_in, 16)
            sp.dma_start(wf_raw[:, :, :], Wf.rearrange("(c p) d -> p c d", p=128)).then_inc(ff_in, 16)

            def load_context(k, buf, first):
                if not first:
                    sp.wait_ge(kd_ready, 8 * (k + A2 - 1))
                    sp.wait_ge(xt_fill, k + A2 - 1)
                src = ctx_in[bass.ds(GB * k, GB), :, :].rearrange("b s d -> s b d")
                for r in (0, 64):
                    sp.dma_start(cx[buf][r:r + 64, :, :], src).then_inc(cx_in[buf], 16)

            load_context(0, 0, True)
            load_context(1, 1, True)
            with sp.Fori(1, NG // 2) as i:
                for c in range(2):
                    load_context(2 * i + c, c, False)

            def store(f):
                sp.wait_ge(fin_add, f + FFK + 1)
                sp.dma_start(ov[:, bass.ds(PP * f, PP), :], xs[:, bass.ds(PP * f, PP), :]).then_inc(out_st, 16)

            with sp.Fori(0, NG) as f:
                store(f)
            sp.wait_ge(out_st, 16 * NG)

        @block.gpsimd
        def _(pool):
            pool.memset(ident[:, :], 0.0).then_inc(id_done, 1)
            pool.wait_ge(id_done, 1)
            pool.affine_select(out=ident[:, :], in_=ident[:, :], compare_op=ALU.not_equal, fill=1.0,
                               base=0, pattern=[[-1, 128]], channel_multiplier=1).then_inc(id_done, 1)
            pool.memset(neghalf[:, :], -0.5).then_inc(consts, 1)
            pool.memset(epsc[:, :], EPS).then_inc(consts, 1)
            pool.memset(one[:, :], 1.0).then_inc(consts, 1)
            for k in range(2):
                for s in range(2):
                    pool.memset(xt[k][s][:, :, :].bitcast(f32), 0.0).then_inc(consts, 1)
            pool.wait_ge(consts, 3)

            def inverse_std(K):
                pool.wait_ge(ln_var, 2 * K + 2)
                pool.tensor_tensor(veps[:, :], mv[:, :, 1], epsc[:, :], ALU.add).then_inc(eps_done, 1)
                pool.wait_ge(eps_done, K + 1)
                pool.tensor_tensor(rstd[:, :], veps[:, :], neghalf[:, :], ALU.pow).then_inc(ln_rstd, 1)

            def gain_offset(K, ln, first=False):
                pool.wait_ge(ln_z, 2 * K + 2)
                gb = gam[:, ln:ln + 1, :].broadcast_to([128, PP, D])
                bb = bet[:, ln:ln + 1, :].broadcast_to([128, PP, D])
                pool.tensor_tensor(xg[:, :, :], xz[:, :, :], gb, ALU.mult).then_inc(xg_done, 1)
                pool.wait_ge(xg_done, K + 1)
                if not first:
                    pool.wait_ge(xt_fill, K)
                pool.tensor_tensor(xn[:, :, :], xg[:, :, :], bb, ALU.add).then_inc(xn_ready, 1)
                if ln == 0:
                    key_hi(K, ln)

            def key_hi(K, ln):
                pool.tensor_tensor(kn[:, :, :].bitcast(f32r), xg[:, :, :],
                                   bet[:, ln:ln + 1, :].broadcast_to([128, PP, D]), ALU.add).then_inc(kn_hi, 1)

            def key_copies(K, buf, a, first=False):
                if not first and known(K) > 1:
                    pool.wait_ge(u_fill, 8 * K - 8)
                if a == 0:
                    pool.wait_ge(kn_hi, K + 1)
                    pool.wait_ge(xn_ready, K + 1)
                    hi, lo = [t[:, :, :].rearrange("r (p b) d -> r p b d", b=2) for t in kd[buf]]
                    n = 0
                    for b in range(2):
                        rows = slice(64 * b, 64 * b + 64)
                        off = bet[rows, 0:1, :].broadcast_to([64, PP, D])
                        for r in (0, 64):
                            pool.tensor_tensor(hi[r:r + 64, :, b, :], xg[rows, :, :], off, ALU.add)\
                                .then_inc(kd_ready, 1)
                            pool.wait_ge(kd_ready, 8 * K + (n + 1))
                            pool.tensor_tensor(lo[r:r + 64, :, b, :], xn[rows, :, :], kn[rows, :, :],
                                               ALU.subtract).then_inc(kd_ready, 1)
                            pool.wait_ge(kd_ready, 8 * K + (n + 2))
                            n += 2
                else:
                    k = K - A2
                    pool.wait_ge(cx_in[buf], 16 * (k - buf) + 32)
                    pool.tensor_tensor(kd[buf][0][:, :, 0:DC], cx[buf][:, :, :],
                                       one[:, :].unsqueeze(2).broadcast_to([128, GB, DC]), ALU.mult).then_inc(kd_hi, 1)
                    pool.wait_ge(kd_hi, k + 1)
                    pool.tensor_tensor(kd[buf][1][:, :, 0:DC], cx[buf][:, :, :],
                                       kd[buf][0][:, :, 0:DC].bitcast(f32), ALU.subtract).then_inc(kd_ready, 8)

            def normalise(K, p, buf=0):
                pool.wait_ge(rs_done, 2 * K + p + 1)
                v = (P1[buf] if p else P0)[:, :].rearrange("r (h s) -> r h s", h=H)
                pool.tensor_tensor(v, v, rs[:, p, :].unsqueeze(2).broadcast_to([128, H, N]), ALU.mult).then_inc(p_norm, 1)

            def centre_scale(K, a):
                v = pairs(K - a * NG)
                if known(K) > 2:
                    pool.wait_ge(xg_done, K)
                pool.tensor_tensor(xz[:, :, :], v, mv[:, :, 0:1].broadcast_to([128, PP, D]),
                                   ALU.subtract).then_inc(ln_c, 1)
                pool.wait_ge(ln_c, K - 1)
                pool.tensor_tensor(xz[:, :, :], xz[:, :, :], rstd[:, :].unsqueeze(2).broadcast_to([128, PP, D]),
                                   ALU.mult).then_inc(ln_z, 2)

            def fold_sums(K, buf):
                pool.wait_ge(exp_1, 2 * K + 2)
                if known(K) > 0:
                    pool.wait_ge(sum_done, K)
                src = P1[buf][:, :].rearrange("r (h s) -> r h s", h=H)
                for i, n in enumerate((32, 16, 8)):
                    pool.tensor_tensor(fold[i][:, :, :], src[:, :, 0:n], src[:, :, n:2 * n],
                                       ALU.add).then_inc(fold_done, 1)
                    if n > 8:
                        pool.wait_ge(fold_done, 3 * K + (i + 1))
                    src = fold[i]

            def step(J, par, a):
                if known(J) < 31:
                    key_copies(J + 1, 1 - par, phase(J + 1, a))
                pool.wait_ge(ln_rstd, J + 3)
                centre_scale(J + 2, phase(J + 2, a))
                gain_offset(J + 2, phase(J + 2, a))
                if known(J) > 0:
                    normalise(J, 1, par)
                if known(J) == 31:
                    ff_weights()
                if known(J) < 31:
                    normalise(J + 1, 0)
                inverse_std(J + 3)
                if known(J) < 31:
                    fold_sums(J + 1, 1 - par)

            inverse_std(0)
            pool.wait_ge(g_in, 32)
            gain_offset(0, 0, True)
            inverse_std(1)
            key_copies(0, 0, 0, True)
            gain_offset(1, 0)
            pool.wait_ge(c_in, 128)
            normalise(0, 0)
            fold_sums(0, 0)
            inverse_std(2)
            normalise(0, 1)

            def ff_weights():
                pool.wait_ge(ffw_hi, 2)
                pool.tensor_tensor(wp[1][:, :], wp_raw[:, :], wp[0][:, :].bitcast(f32),
                                   ALU.subtract).then_inc(ffw_lo, 1)
                pool.tensor_tensor(wf[1][:, :, :], wf_raw[:, :, :], wf[0][:, :, :].bitcast(f32),
                                   ALU.subtract).then_inc(ffw_lo, 1)

            steps(pool, step)
            pool.wait_ge(ln_rstd, 35)
            centre_scale(34, 2)
            gain_offset(34, 2)
            inverse_std(35)

            def y_rest(f, par):
                pool.wait_ge(y_hi, 2 * f + 2)
                h = slice(NCH // 2, NCH)
                pool.tensor_tensor(yh[par][1][:, h, :], yf[par][:, h, :], yh[par][0][:, h, :].bitcast(f32),
                                   ALU.subtract).then_inc(y_lo_2, 1)

            def ff_step(f, par, apply=True, stat=True):
                if apply:
                    gain_offset(f + (FFK + 3), 2)
                y_rest(f, par)
                if stat:
                    inverse_std(f + (FFK + 4))

            with pool.Fori(0, 6) as i:
                for c in range(2):
                    ff_step(2 * i + c, c)
            ff_step(12, 0, stat=False)
            for f in range(13, 16):
                ff_step(f, f % 2, apply=False, stat=False)

        @block.scalar
        def _(act):
            def prepare(a, banks):
                plan = prep_plan(a)
                for i in banks:
                    kind, n, dst = plan[i]
                    m = 14 * a + i
                    bank = prep_bank(m)
                    act.wait_ge(prep_fill, m + 1)
                    if kind == "T":
                        act.activation(dst[:, n:n + 2, 0:DKW(a, i)],
                                       bank[:, 0:2 * DKW(a, i)].rearrange("p (h d) -> p h d", h=2),
                                       ACT.Copy).then_inc(prep_a, 1)
                    else:
                        act.activation(dst[0][0:DK[a], n:n + 7:2, :],
                                       bank[0:DK[a], :].rearrange("p (h d) -> p h d", h=4),
                                       ACT.Copy).then_inc(prep_a, 1)

            def xt_half(K, par, a, bank, first=False):
                act.wait_ge(xt_fill, K + 1)
                if not first:
                    act.wait_ge(s_fill, 4 * K - 4)
                act.activation(batches(xt[par][0]), bank[:, 0:GT].rearrange("d (p q c) -> d p q c", q=2, c=64),
                               ACT.Copy).then_inc(xt_hi, 1)
                if a == 1:
                    act.wait_ge(t_fill, 8 * K)
                    act.activation(ct[0][0:DC, :], bank[0:DC, GT:2 * GT], ACT.Copy).then_inc(ct_hi, 1)

            def t_half(K, a, first=False):
                for i in range(TF):
                    act.wait_ge(t_fill, 8 * K + (i + 1))
                    if not first and i == 0:
                        act.wait_ge(s_fill, 4 * K)
                    bank = first_t_bank(K, i) if first else (8 + i) % 5
                    act.activation(T[0][:, :, 2 * i:2 * i + 2, :].rearrange("d b h s -> d h b s"),
                                   ring[bank][:, :].rearrange("d (h b s) -> d h b s", h=2, b=GB),
                                   ACT.Copy).then_inc(t_hi, 1)

            def exps_0(K, first=False):
                for h in range(H):
                    if h % HP == 0:
                        act.wait_ge(nmx_done, 2 * K + (h // HP + 1))
                    if h == 0 and not first:
                        act.wait_ge(pt_fill, 4 * K - 2)
                        act.wait_ge(rs_done, 2 * K - 1)
                    act.activation(P0[:, N * h:N * h + N], ps_s[h // HP][:, N * (h % HP):N * (h % HP) + N],
                                   ACT.Exp, bias=nmx[:, h:h + 1], scale=SCALE,
                                   accum_out=sm[:, 0, h:h + 1]).then_inc(exp_0, 1)

            def exps_1(K, buf, halves=(0, 1)):
                for h in halves:
                    act.wait_ge(s_sub, 2 * K + (h + 1))
                    v = P1[buf][:, HALF * h:HALF * h + HALF]
                    act.activation(v, v, ACT.Exp, scale=SCALE).then_inc(exp_1, 1)

            def pt_half(K, p, first=False):
                for q in range(2):
                    act.wait_ge(pt_fill, 4 * K + (2 * p + q + 1))
                    if q == 0 and not (first and p == 0):
                        act.wait_ge(u_fill, 8 * K + 4 * p)
                    src = ring[(6 * p + q) % 5][:, :].rearrange("r (h c) -> r h c", h=4)
                    if p == 1:
                        act.activation(pt[:, 4 * q:4 * q + 4, 0, :], src, ACT.Copy).then_inc(pt_hi, 1)
                        continue
                    for e, r in ((0, 0), (1, 64)):
                        act.activation(pt[r:r + 64, 4 * q:4 * q + 4, e, :], src[r:r + 64, :, :],
                                       ACT.Copy).then_inc(pt_hi, 1)

            def u_half(K, p, a, first=False):
                for c in range(4):
                    act.wait_ge(u_fill, 8 * K + (4 * p + c + 1))
                    if c == 0 and p == 0 and not first:
                        act.wait_ge(o_fill, K)
                    act.activation(u_dst(0, p, c, a), u_src(p, c, a), ACT.Copy).then_inc(u_hi, 1)

            def out_copy(K, a, src):
                act.wait_ge(o_fill, K + 1)
                if not (isinstance(K, int) and K == 0):
                    act.wait_ge(fin_fill, K)
                act.activation(oT[:, :], src, ACT.Identity, bias=bo_col[:, a:a + 1]).then_inc(o_out, 1)

            def step(J, par, a):
                pt_half(J, 0, known(J) == 0)
                if known(J) < 31:
                    exps_0(J + 1)
                    exps_1(J + 1, 1 - par, (0,))
                xt_half(J + 2, par, phase(J + 2, a), ps_s[0])
                if known(J) > 0:
                    out_copy(J - 1, phase(J - 1, a), ps_m[:, 0:GT])
                u_half(J, 0, phase(J, a), known(J) == 0)
                if known(J) < 31:
                    exps_1(J + 1, 1 - par, (1,))
                pt_half(J, 1)
                if known(J) < 30:
                    t_half(J + 2, phase(J + 2, a))
                u_half(J, 1, phase(J, a))

            prepare(0, range(10))
            act.wait_ge(consts, 7)
            xt_half(0, 0, 0, ps_m, True)
            t_half(0, 0, True)
            xt_half(1, 1, 0, ps_m, True)
            prepare(0, range(10, 14))
            act.wait_ge(c_in, 128)
            exps_0(0, True)
            prepare(1, range(6))
            exps_1(0, 0)
            prepare(1, range(6, 14))
            t_half(1, 0, True)

            def ff_weights():
                act.wait_ge(ff_in, 32)
                act.wait_ge(s_fill, 4 * FFK)
                act.activation(wp[0][:, :], wp_raw[:, :], ACT.Copy).then_inc(ffw_hi, 1)
                act.activation(wf[0][:, :, :], wf_raw[:, :, :], ACT.Copy).then_inc(ffw_hi, 1)

            steps(act, step, ff_weights)

            def ff_xt(K, par):
                act.wait_ge(xt_fill, K + 1)
                act.activation(batches(xt[par][0]), ring[2][:, 0:GT].rearrange("d (p q c) -> d p q c", q=2, c=64),
                               ACT.Copy).then_inc(xt_hi, 1)

            def gelus(f, first=False):
                for c in range(NCH):
                    act.wait_ge(gate_fill, 2 * f + (c // 2 + 1))
                    if not first:
                        act.wait_ge(y_done, 4 * f - (3 - c))
                    act.activation(gel[:, c, :], ps_s[c // 2][:, GT * (c % 2):GT * (c % 2) + GT], ACT.Gelu,
                                   bias=bp_col[:, NCH + c:NCH + c + 1]).then_inc(gel_done, 1)

            def y_half(f, par):
                for i in range(2):
                    act.wait_ge(y_done, 4 * f + (2 * i + 2))
                    if i == 0:
                        act.wait_ge(o_fill, f + (FFK - 1))
                    h = slice(2 * i, 2 * i + 2)
                    act.activation(yh[par][0][:, h, :], yf[par][:, h, :], ACT.Copy).then_inc(y_hi, 1)

            def ff_step(f, par, first=False, turn=True, up=True):
                if up:
                    gelus(f, first)
                if turn:
                    ff_xt(f + (FFK + 2), par)
                if up:
                    y_half(f, par)
                if first:
                    out_copy(FFK - 1, 1, ps_m[:, 0:GT])
                else:
                    out_copy(f + (FFK - 1), 2, ring[3][:, 0:GT])

            ff_step(0, 0, True)
            ff_step(1, 1)
            with act.Fori(0, 6) as i:
                for c in range(2):
                    ff_step(2 * i + (c + 2), c)
            ff_step(14, 0, turn=False)
            ff_step(15, 1, turn=False)
            ff_step(16, 0, turn=False, up=False)

        @block.vector
        def _(dve):
            def prepare(a, banks):
                plan = prep_plan(a)
                for i in banks:
                    kind, n, dst = plan[i]
                    m = 14 * a + i
                    bank = prep_bank(m)
                    dve.wait_ge(prep_a, m + 1)
                    if kind == "T":
                        w = DKW(a, i)
                        dve.tensor_copy(dst[:, n + 2:n + 4, 0:w],
                                        bank[:, 2 * w:4 * w].rearrange("p (h d) -> p h d", h=2))\
                            .then_inc(prep_v, 1)
                    else:
                        dve.tensor_tensor(dst[1][0:DK[a], n:n + 7:2, :],
                                          bank[0:DK[a], :].rearrange("p (h d) -> p h d", h=4),
                                          dst[0][0:DK[a], n:n + 7:2, :].bitcast(f32), ALU.subtract)\
                            .then_inc(prep_v, 1)

            def xrow(K, a, p):
                return xs[:, bass.ds(PP * (K - a * NG) + p, 1), :].rearrange("r o d -> r (o d)")

            def norm_stats(K, a):
                if a > 0:
                    dve.wait_ge(fin_add, K - (NG - 1))
                for p in range(PP):
                    dve.bn_stats(stats[:, p, :], xrow(K, a, p)).then_inc(st_done, 1)

            def norm_aggregate(K):
                for p in range(PP):
                    dve.bn_aggr(mv[:, p, :], stats[:, p, :]).then_inc(ln_var, 1)

            def norm_apply(K, a, first=False):
                dve.wait_ge(ln_rstd, K + 1)
                if not first:
                    dve.wait_ge(xg_done, K)
                for p in range(PP):
                    dve.tensor_scalar(xz[:, p, :], xrow(K, a, p), mv[:, p, 0:1], rstd[:, p:p + 1],
                                      ALU.subtract, ALU.mult).then_inc(ln_z, 1)

            def xt_rest(K, par, a, src):
                dve.wait_ge(xt_hi, K + 1)
                if a == 1:
                    dve.wait_ge(ct_hi, K - (A2 - 1))
                dve.tensor_tensor(batches(xt[par][1]), src[:, 0:GT].rearrange("d (p q c) -> d p q c", q=2, c=64),
                                  batches(xt[par][0]).bitcast(f32),
                                  ALU.subtract).then_inc(xt_lo, 1)
                if a == 1:
                    dve.tensor_tensor(ct[1][0:DC, :], src[0:DC, GT:2 * GT], ct[0][0:DC, :].bitcast(f32),
                                      ALU.subtract).then_inc(ct_lo, 1)

            def t_rest(K, first=False):
                for i in range(TF):
                    dve.wait_ge(t_hi, 8 * K + (i + 1))
                    bank = first_t_bank(K, i) if first else (8 + i) % 5
                    dst = [t[:, :, 2 * i:2 * i + 2, :].rearrange("d b h s -> d h b s") for t in T]
                    dve.tensor_tensor(dst[1], ring[bank][:, :].rearrange("d (h b s) -> d h b s", h=2, b=GB),
                                      dst[0].bitcast(f32), ALU.subtract).then_inc(t_lo, 1)

            def maxes_0(K, first=False):
                for h in range(2):
                    dve.wait_ge(s_fill, 4 * K + (h + 1))
                    m = mx[:, 0, HP * h:HP * h + HP]
                    dve.tensor_reduce(m, ps_s[h][:, :].rearrange("r (h s) -> r h s", s=N), AX.X,
                                      ALU.max).then_inc(mx_done, 1)
                    dve.wait_ge(mx_done, 4 * K + (h + 1))
                    dve.tensor_scalar(nmx[:, HP * h:HP * h + HP], m, -SCALE, None, ALU.mult).then_inc(nmx_done, 1)

            def maxes_1(K, buf):
                for h in range(2):
                    dve.wait_ge(s_fill, 4 * K + (h + 3))
                    v = ps_s[h][:, :].rearrange("r (h s) -> r h s", s=N)
                    m = mx[:, 1, HP * h:HP * h + HP]
                    dve.tensor_reduce(m, v, AX.X, ALU.max).then_inc(mx_done, 1)
                    dve.wait_ge(mx_done, 4 * K + (h + 3))
                    dve.tensor_tensor(P1[buf][:, HALF * h:HALF * h + HALF].rearrange("r (h s) -> r h s", s=N), v,
                                      m.unsqueeze(2).broadcast_to([128, HP, N]), ALU.subtract).then_inc(s_sub, 1)

            def inverse_0(K):
                dve.wait_ge(exp_0, H * K + H)
                dve.reciprocal(rs[:, 0, :], sm[:, 0, :]).then_inc(rs_done, 1)

            def sums_1(K):
                dve.wait_ge(fold_done, 3 * K + 3)
                dve.tensor_reduce(sm[:, 1, :], fold[2][:, :, :], AX.X, ALU.add).then_inc(sum_done, 1)
                dve.wait_ge(sum_done, K + 1)
                dve.reciprocal(rs[:, 1, :], sm[:, 1, :]).then_inc(rs_done, 1)

            def pt_rest(K, p):
                for q in range(2):
                    src = ring[(6 * p + q) % 5][:, :].rearrange("r (h c) -> r h c", h=4)
                    if p == 1:
                        dve.wait_ge(pt_hi, 6 * K + (q + 5))
                        dve.tensor_tensor(pt[:, 4 * q:4 * q + 4, 1, :], src,
                                          pt[:, 4 * q:4 * q + 4, 0, :].bitcast(f32), ALU.subtract).then_inc(pt_lo, 1)
                        continue
                    for e, r in ((0, 0), (1, 64)):
                        dve.wait_ge(pt_hi, 6 * K + (2 * q + e + 1))
                        dve.tensor_tensor(pt[64 - r:128 - r, 4 * q:4 * q + 4, e, :], src[r:r + 64, :, :],
                                          pt[r:r + 64, 4 * q:4 * q + 4, e, :].bitcast(f32),
                                          ALU.subtract).then_inc(pt_lo, 1)

            def u_rest(K, p, a, banks=range(4)):
                for c in banks:
                    dve.wait_ge(u_hi, 8 * K + (4 * p + c + 1))
                    dve.tensor_tensor(u_dst(1, p, c, a), u_src(p, c, a), u_dst(0, p, c, a).bitcast(f32),
                                      ALU.subtract).then_inc(u_lo, 1)

            def fin(K, a, src):
                dve.wait_ge(fin_fill, K + 1)
                v = pairs(K - a * NG)
                dve.tensor_tensor(v, src[:, 0:GT].rearrange("r (p d) -> r p d", p=PP), v, ALU.add)\
                    .then_inc(fin_add, 1)

            def step(J, par, a):
                if known(J) < 31:
                    maxes_0(J + 1)
                if known(J) > 0:
                    sums_1(J)
                pt_rest(J, 0)
                if known(J) < 31:
                    maxes_1(J + 1, 1 - par)
                xt_rest(J + 2, par, phase(J + 2, a), ps_s[0])
                dve.wait_ge(ln_z, 2 * J + 6)
                norm_stats(J + 3, phase(J + 3, a))
                dve.wait_ge(st_done, 2 * J + 8)
                if known(J) < 31:
                    inverse_0(J + 1)
                norm_aggregate(J + 3)
                u_rest(J, 0, phase(J, a), range(2))
                if known(J) > 0:
                    fin(J - 1, phase(J - 1, a), ps_m)
                u_rest(J, 0, phase(J, a), range(2, 4))
                pt_rest(J, 1)
                if known(J) < 30:
                    t_rest(J + 2)
                u_rest(J, 1, phase(J, a))

            def norm_first(g):
                dve.wait_ge(x_in[g], 16)
                norm_stats(g, 0)
                dve.wait_ge(st_done, 2 * g + 2)
                norm_aggregate(g)

            norm_first(0)
            prepare(0, range(1))
            norm_apply(0, 0, True)
            norm_first(1)
            prepare(0, range(1, 10))
            xt_rest(0, 0, 0, ps_m)
            norm_apply(1, 0)
            t_rest(0, True)
            xt_rest(1, 1, 0, ps_m)
            prepare(0, range(10, 14))
            maxes_0(0, True)
            maxes_1(0, 0)
            prepare(1, range(6))
            inverse_0(0)
            norm_first(2)
            prepare(1, range(6, 14))
            sums_1(0)
            t_rest(1, True)
            dve.wait_ge(x_in[3], 16)
            steps(dve, step)
            norm_stats(35, 2)
            dve.wait_ge(st_done, 2 * 35 + 2)
            dve.wait_ge(ln_z, 2 * 34 + 2)
            norm_aggregate(35)

            def products(f, par, first=False):
                for c in range(NCH):
                    dve.wait_ge(gel_done, 4 * f + (c + 1))
                    dve.wait_ge(a_fill, 2 * f + (c // 2 + 1))
                    if not first and c == 0:
                        dve.wait_ge(y_hi, 2 * f - 2)
                        dve.wait_ge(y_lo, f - 1)
                        dve.wait_ge(y_lo_2, f - 1)
                    dve.scalar_tensor_tensor(yf[par][:, c, :], ring[c // 2][:, GT * (c % 2):GT * (c % 2) + GT],
                                             bp_col[:, c:c + 1], gel[:, c, :], ALU.add, ALU.mult)\
                        .then_inc(y_done, 1)

            def y_rest(f, par):
                dve.wait_ge(y_hi, 2 * f + 1)
                h = slice(0, NCH // 2)
                dve.tensor_tensor(yh[par][1][:, h, :], yf[par][:, h, :], yh[par][0][:, h, :].bitcast(f32),
                                  ALU.subtract).then_inc(y_lo, 1)

            def ff_step(f, par, first=False, second=False, up=True, turn=True, apply=True, stat=True, rest=True):
                if not first and rest:
                    y_rest(f - 1, 1 - par)
                if up:
                    products(f, par, first or second)
                if apply:
                    norm_apply(f + (FFK + 3), 2)
                if stat:
                    norm_stats(f + (FFK + 4), 2)
                    dve.wait_ge(st_done, 2 * f + (2 * FFK + 10))
                if turn:
                    xt_rest(f + (FFK + 2), par, 2, ring[2])
                if second:
                    fin(FFK - 1, 1, ps_m)
                elif not first:
                    fin(f + (FFK - 2), 2, ring[4])
                if stat:
                    norm_aggregate(f + (FFK + 4))

            ff_step(0, 0, first=True)
            ff_step(1, 1, second=True)
            with dve.Fori(0, 5) as i:
                for c in range(2):
                    ff_step(2 * i + (c + 2), c)
            ff_step(12, 0, stat=False)
            ff_step(13, 1, apply=False, stat=False)
            ff_step(14, 0, turn=False, apply=False, stat=False)
            ff_step(15, 1, turn=False, apply=False, stat=False)
            ff_step(16, 0, up=False, turn=False, apply=False, stat=False)
            ff_step(17, 1, up=False, turn=False, apply=False, stat=False, rest=False)

        @block.tensor
        def _(pe):
            def prepare(a, banks):
                plan = prep_plan(a)
                for i in banks:
                    kind, n, dst = plan[i]
                    m = 14 * a + i
                    if 10 <= m < 15:
                        pe.wait_ge(t_lo, m - 6)
                    elif m >= 5:
                        pe.wait_ge(prep_v, m - 4)
                    bank = prep_bank(m)
                    if kind == "T":
                        w = i // 2
                        pe.wait_ge(w_in[a][w], 16)
                        d = DKW(a, i)
                        for j in range(4):
                            last = pe.transpose(bank[:, d * j:d * j + d],
                                                wst[a][w][0:d, 128 * (n + j):128 * (n + j) + 128],
                                                ident[0:d, 0:d])
                    else:
                        if i == 6:
                            pe.wait_ge(prep_v, 14 * a + 4)
                        if i == 10:
                            pe.wait_ge(prep_v, 14 * a + 6)
                            pe.wait_ge(w_in[a][3], 16)
                        left = wT[a][0 if kind == "A" else 2]
                        right = wT[a][1] if kind == "A" else wo_st[a]
                        for j in range(4):
                            hp, r = (n + 2 * j) // 2, 64 * (n % 2)
                            last = pe.matmul(bank[0:DK[a], 128 * j:128 * j + 128], left[r:r + 64, hp, 0:DK[a]],
                                             right[r:r + 64, hp, :], start=True, stop=True)
                    last.then_inc(prep_fill, 1)

            def turn(K, par, a, bank, first=False):
                if a == 1:
                    k = K - A2
                    pe.wait_ge(cx_in[par], 16 * (k - par) + 32)
                pe.wait_ge(xn_ready, K + 1)
                if first:
                    if K > 0:
                        pe.wait_ge(xt_lo, K)
                elif known(K) == FFK + 1:
                    pe.wait_ge(xt_lo, K)
                else:
                    pe.wait_ge(s_sub, 2 * K - 1)
                for p in range(PP):
                    last = pe.transpose(bank[:, 128 * p:128 * p + 128], xn[:, p, :], ident[:, :])
                if a == 1:
                    for b in range(GB):
                        last = pe.transpose(bank[0:DC, GT + N * b:GT + N * b + N], cx[par][0:64, b, :],
                                            ident[0:64, 0:64])
                last.then_inc(xt_fill, 1)

            def t_products(K, par, a, first=False):
                pe.wait_ge(xt_lo, K + 1)
                if a == 1:
                    pe.wait_ge(ct_lo, K - (A2 - 1))
                mov = [batches(t) for t in xt[par]] if a == 0 else [t[0:DC, :] for t in ct]
                for i in range(TF):
                    if first:
                        bank = first_t_bank(K, i)
                        if i >= 5:
                            pe.wait_ge(t_lo, 8 * K + i - 4)
                        else:
                            pe.wait_ge(prep_v, (6 if K == 0 else 24) + i)
                    else:
                        bank = (8 + i) % 5
                        if i < 3:
                            pe.wait_ge(u_lo, 8 * (K - 2) + (i + 2))
                        elif i < 5:
                            pe.wait_ge(pt_lo, 6 * (K - 2) + (i + 2))
                        else:
                            pe.wait_ge(t_lo, 8 * K + (i - 4))
                    for j in range(2):
                        o = ring[bank][:, GT * j:GT * j + GT]
                        for n, (s, m) in enumerate(PARTS):
                            last = pe.matmul(o, AW[a][s][0:DK[a], 2 * i + j, :], mov[m],
                                             start=(n == 0), stop=(n == 2))
                    last.then_inc(t_fill, 1)

            def scores(K, p, par, first=False, halves=(0, 1)):
                if p == 0:
                    pe.wait_ge(t_lo, 8 * K + 8)
                for h in halves:
                    if p == 1:
                        pe.wait_ge(exp_0, H * K + HP * (h + 1))
                    elif not first:
                        pe.wait_ge(s_sub, 2 * K + (h - 1))
                    n = 0
                    for b in range(2):
                        for s, m in PARTS:
                            last = pe.matmul(ps_s[h][:, :], xt[par][s][:, p, 128 * b:128 * b + 128],
                                             T[m][:, 2 * p + b, 8 * h:8 * h + 8, :].rearrange("d h s -> d (h s)"),
                                             start=(n == 0), stop=(n == 5))
                            n += 1
                    last.then_inc(s_fill, 1)

            def turn_softmax(K, p, buf=0, with_t=True):
                pe.wait_ge(p_norm, 2 * K + (p + 1))
                if p == 0 and with_t:
                    pe.wait_ge(t_lo, 8 * K + 16)
                for q in range(2):
                    if p == 1 and q == 1:
                        pe.wait_ge(u_lo, 8 * K + 1)
                    if p == 0 and q == 1 and known(K) > 0:
                        pe.wait_ge(u_lo, 8 * K - 3)
                    for j in range(4):
                        hp = 4 * q + j
                        last = pe.transpose(ring[(6 * p + q) % 5][:, 128 * j:128 * j + 128],
                                            (P1[buf] if p else P0)[:, 128 * hp:128 * hp + 128], ident[:, :])
                    last.then_inc(pt_fill, 1)

            def u_products(K, p, par, a, with_t=True, banks=range(4)):
                pe.wait_ge(pt_lo, 6 * K + (2 * p + 4))
                pe.wait_ge(kd_ready, 8 * K + 8)
                for c in banks:
                    b, e = c // 2, c % 2
                    r = 64 * e
                    if p == 1:
                        if with_t:
                            pe.wait_ge(t_lo, 8 * (K + 2) + (c + 4))
                        elif c == 0:
                            pe.wait_ge(u_lo, 8 * K + 4)
                    o = u_src(p, c, a).rearrange("d h n -> d (h n)")
                    if p == 1:
                        for n, (s, m) in enumerate(PARTS):
                            last = pe.matmul(o, kd[par][s][r:r + 64, 2 * p + b, 0:DK[a]],
                                             pt[r:r + 64, :, m, 64 * b:64 * b + 64], start=(n == 0), stop=(n == 2))
                        last.then_inc(u_fill, 1)
                        continue
                    pe.matmul(o, kd[par][0][:, 2 * p + b, 0:DK[a]], pt[:, :, e, 64 * b:64 * b + 64],
                              start=True, stop=False)
                    last = pe.matmul(o, kd[par][1][r:r + 64, 2 * p + b, 0:DK[a]],
                                     pt[r:r + 64, :, e, 64 * b:64 * b + 64], start=False, stop=True)
                    last.then_inc(u_fill, 1)

            def out_products(K, a, heads=range(H)):
                if heads[0] == 0:
                    pe.wait_ge(u_lo, 8 * K + 8)
                n = 3 * heads[0]
                for h in heads:
                    for s, m in PARTS:
                        last = pe.matmul(ps_m[:, 0:GT], OW[a][s][0:DK[a], h, :], U[m][0:DK[a], h, :],
                                         start=(n == 0), stop=(n == 3 * H - 1))
                        n += 1
                if heads[-1] == H - 1:
                    last.then_inc(o_fill, 1)

            def turn_back(K, bank):
                pe.wait_ge(o_out, K + 1)
                for p in range(PP):
                    last = pe.transpose(bank[:, 128 * p:128 * p + 128], oT[:, 128 * p:128 * p + 128], ident[:, :])
                last.then_inc(fin_fill, 1)

            def step(J, par, a):
                turn_softmax(J, 0, with_t=known(J) < 31)
                if known(J) < 31:
                    scores(J + 1, 0, 1 - par)
                for heads in OUT_SPLIT:
                    if known(J) > 0:
                        out_products(J - 1, phase(J - 1, a), heads)
                    if known(J) < 31 and heads[-1] < H - 1:
                        scores(J + 1, 1, 1 - par, halves=(0,) if heads[0] == 0 else (1,))
                    if heads == OUT_SPLIT[1]:
                        turn(J + 2, par, phase(J + 2, a), ps_s[0])
                u_products(J, 0, par, phase(J, a), banks=range(2))
                if known(J) > 0:
                    turn_back(J - 1, ps_m)
                u_products(J, 0, par, phase(J, a), banks=range(2, 4))
                turn_softmax(J, 1, par)
                if known(J) < 30:
                    t_products(J + 2, par, phase(J + 2, a))
                if known(J) == 31:
                    up_products(0, 0, range(NCH), True)
                u_products(J, 1, par, phase(J, a), known(J) < 30)

            def up_products(f, par, chunks=range(2 * NCH), first=False):
                K = f + FFK
                if first:
                    pe.wait_ge(ffw_lo, 2)
                pe.wait_ge(xt_lo, K + 1)
                mov = [batches(t) for t in xt[par]]
                for c in chunks:
                    gate = c < NCH
                    i, j = (c % NCH) // 2, c % 2
                    if j == 0:
                        if gate and first:
                            if i == 0:
                                pe.wait_ge(xt_lo, K + 2)
                            else:
                                pe.wait_ge(s_sub, 2 * FFK)
                        elif first:
                            pe.wait_ge(u_lo, 8 * FFK - 4 + i)
                        elif gate:
                            pe.wait_ge(gel_done, 4 * f - (2 - 2 * i))
                        else:
                            pe.wait_ge(y_done, 4 * f - (2 - 2 * i))
                    o = (ps_s if gate else ring)[i][:, GT * j:GT * j + GT]
                    col = 128 * (c % NCH) + (FF if gate else 0)
                    for n, (s, m) in enumerate(PARTS):
                        last = pe.matmul(o, wp[s][:, col:col + 128], mov[m], start=(n == 0), stop=(n == 2))
                    if j == 1:
                        last.then_inc(gate_fill if gate else a_fill, 1)

            def down_products(f, par):
                K = f + FFK
                pe.wait_ge(y_lo, f + 1)
                pe.wait_ge(y_lo_2, f + 1)
                pe.wait_ge(o_out, K)
                n = 0
                for c in range(NCH):
                    for s, m in PARTS:
                        last = pe.matmul(ring[3][:, 0:GT], wf[s][:, c, :], yh[par][m][:, c, :],
                                         start=(n == 0), stop=(n == 3 * NCH - 1))
                        n += 1
                last.then_inc(o_fill, 1)

            def ff_turn(K, first=False):
                pe.wait_ge(xn_ready, K + 1)
                if first:
                    pe.wait_ge(u_lo, 8 * FFK - 2)
                else:
                    pe.wait_ge(xt_lo, K)
                for p in range(PP):
                    last = pe.transpose(ring[2][:, 128 * p:128 * p + 128], xn[:, p, :], ident[:, :])
                last.then_inc(xt_fill, 1)

            def ff_step(f, par, up=True, turn=True, down=True):
                if up:
                    up_products(f, par)
                if turn:
                    ff_turn(f + (FFK + 2))
                K = f + (FFK - 2)
                pe.wait_ge(fin_add, K)
                turn_back(K, ring[4])
                if down:
                    down_products(f - 1, 1 - par)

            pe.wait_ge(id_done, 2)
            prepare(0, range(10))
            turn(0, 0, 0, ps_m, True)
            pe.wait_ge(prep_v, 10)
            t_products(0, 0, 0, 1)
            turn(1, 1, 0, ps_m, True)
            prepare(0, range(10, 14))
            scores(0, 0, 0, True)
            prepare(1, range(5))
            scores(0, 1, 0)
            prepare(1, range(5, 14))
            t_products(1, 1, 0, 1)
            steps(pe, step)

            up_products(0, 0, range(NCH, 2 * NCH), True)
            ff_turn(FFK + 2, True)
            out_products(FFK - 1, 1)
            up_products(1, 1)
            ff_turn(FFK + 3)
            turn_back(FFK - 1, ps_m)
            down_products(0, 0)
            with pe.Fori(0, 6) as i:
                for c in range(2):
                    ff_step(2 * i + (c + 2), c)
            ff_step(14, 0, turn=False)
            ff_step(15, 1, turn=False)
            ff_step(16, 0, up=False, turn=False)
            ff_step(17, 1, up=False, turn=False, down=False)


_INS = ["x", "ctx_768"] + [f"L0_xattn_{n}" for n in
        ("Wq1", "Wk1", "Wv1", "Wo1", "bo1", "Wq2", "Wk2", "Wv2", "Wo2", "bo2", "Wp", "bp", "Wf", "bf",
         "g1", "b1", "g2", "b2", "g3", "b3")]


def kernel(**inputs):
    import numpy as _np
    import concourse.bacc as _bacc
    from concourse import mybir as _mybir
    from concourse.bass_utils import run_bass_kernel_spmd as _run

    nc = _bacc.Bacc("TRN2", target_bir_lowering=False, num_devices=1)
    arrays, args = {}, []
    for name in _INS:
        a = _np.ascontiguousarray(inputs[name])
        arrays[f"in_{name}"] = a
        args.append(nc.dram_tensor(f"in_{name}", a.shape, _mybir.dt.from_np(a.dtype), kind="ExternalInput").ap())
    o = nc.dram_tensor("out", arrays["in_x"].shape, _mybir.dt.from_np(arrays["in_x"].dtype),
                       kind="ExternalOutput").ap()
    xattn_block(nc, *args, o)
    r = _run(nc, [arrays], core_ids=[0])
    return r.results[0]["out"]
```
